# Optimizing a Trainium2 kernel written in Bass

```python
import numpy as np
import jax
import jax.numpy as jnp

def _softmax(x, axis=-1):
    return jax.nn.softmax(x, axis=axis)

def _gelu(x):
    return jax.nn.gelu(x, approximate=True)

def _silu(x):
    return jax.nn.silu(x)

def _sigmoid(x):
    return jax.nn.sigmoid(x)

def _layernorm(x, axis=-1, eps=1e-05):
    m = jnp.mean(x, axis=axis, keepdims=True)
    v = jnp.var(x, axis=axis, keepdims=True)
    return (x - m) / jnp.sqrt(v + eps)

def _scatter_add(tgt, idx, src, axis=0):
    return tgt.at[idx].add(src)

def _segment_sum(src, seg, n):
    return jax.ops.segment_sum(src, seg, n)
kernel_name = 'mk_seq_preln_d1_jaxref_r8_71755c'

def setup_inputs(seed: int=0):
    np.random.seed(seed)
    _w = jnp.asarray

    def _L0_attn_setup():
        import jax, jax.numpy as jnp
        import numpy as np
        B, S, D, H = (2, 256, 128, 16)
        HD = D // H
        key = jax.random.key(seed)
        ks = jax.random.split(key, 16)
        sc = 0.02
        return {'hidden_states': jax.random.normal(ks[0], (B, S, D), jnp.float32), 'Wq': jax.random.normal(ks[1], (D, D), jnp.float32) * sc, 'bq': jnp.zeros((D,), jnp.float32), 'Wk': jax.random.normal(ks[2], (D, D), jnp.float32) * sc, 'bk': jnp.zeros((D,), jnp.float32), 'Wv': jax.random.normal(ks[3], (D, D), jnp.float32) * sc, 'bv': jnp.zeros((D,), jnp.float32), 'Wo': jax.random.normal(ks[4], (D, D), jnp.float32) * sc, 'bo': jnp.zeros((D,), jnp.float32), 'rel_W': jax.random.normal(ks[5], (3, 2 * D), jnp.float32) * sc, 'rel_b': jnp.zeros((3,), jnp.float32), 'logical_bias': jax.random.normal(ks[6], (H, 3), jnp.float32) * sc, 'gate_W': jax.random.normal(ks[7], (H, D), jnp.float32) * sc, 'gate_b': jnp.zeros((H,), jnp.float32)}
    _L0_attn_in = _L0_attn_setup()

    def _L0_ffn_setup():
        import jax, jax.numpy as jnp
        import numpy as np
        DIM = 128
        DEPTH = 6
        HEADS = 16
        DIM_HEAD = 64
        WINDOW = 32
        INNER = HEADS * DIM_HEAD
        DIM_INNER = int(DIM * 4 * 2 / 3)
        QK_SCALE = 8.0

        def shift_tokens(t):
            a, s = jnp.split(t, 2, -1)
            s = jnp.pad(s, ((0, 0), (1, 0), (0, 0)))[:, :-1]
            return jnp.concatenate([a, s], -1)

        def l2norm(t):
            return t / jnp.maximum(jnp.linalg.norm(t, axis=-1, keepdims=True), 1e-12)

        def rotate_half(x):
            x1, x2 = jnp.split(x, 2, -1)
            return jnp.concatenate([-x2, x1], -1)

        def rotary_tables(n):
            half = jnp.arange(0, DIM_HEAD, 2, dtype=jnp.float32)
            inv_freq = 1.0 / 10000.0 ** (half / DIM_HEAD)
            t = jnp.arange(n, dtype=jnp.float32)
            freqs = t[:, None] * inv_freq[None, :]
            freqs = jnp.concatenate([freqs, freqs], -1)
            base_scale = (half + 0.4 * DIM_HEAD) / (1.4 * DIM_HEAD)
            power = (t - n // 2) / (WINDOW // 2)
            scale = base_scale[None, :] ** power[:, None]
            scale = jnp.concatenate([scale, scale], -1)
            return (freqs, scale)

        def local_attention(q, k, v):
            b, h, n, d = q.shape
            w = WINDOW
            nw = n // w
            bq = q.reshape(b, h, nw, w, d)
            bk = k.reshape(b, h, nw, w, d)
            bv = v.reshape(b, h, nw, w, d)

            def look(t):
                p = jnp.pad(t, ((0, 0), (0, 0), (1, 0), (0, 0), (0, 0)))
                return jnp.concatenate([p[:, :, :nw], p[:, :, 1:]], axis=3)
            bk2, bv2 = (look(bk), look(bv))
            seq = jnp.arange(n).reshape(nw, w)
            seq_p = jnp.pad(seq, ((1, 0), (0, 0)), constant_values=-1)
            jt = jnp.concatenate([seq_p[:nw], seq_p[1:]], axis=1)
            it = seq[:, :, None]
            jb = jt[:, None, :]
            mask = (it < jb) | (it > jb + w) | (jb == -1)
            sim = jnp.einsum('bhwie,bhwje->bhwij', bq, bk2) * QK_SCALE
            sim = jnp.where(mask, -jnp.finfo(sim.dtype).max, sim)
            attn = jax.nn.softmax(sim, -1)
            out = jnp.einsum('bhwij,bhwje->bhwie', attn, bv2)
            return out.reshape(b, h, n, d)

        def attn_layer(x, Wqkv, qs, ksc, Wo):
            b, n, _ = x.shape
            qkv = x @ Wqkv
            q, k, v = jnp.split(qkv, 3, -1)
            sh = lambda t: t.reshape(b, n, HEADS, DIM_HEAD).transpose(0, 2, 1, 3)
            q, k, v = (sh(q), sh(k), sh(v))
            q = l2norm(q) * qs
            k = l2norm(k) * ksc
            freqs, scale = rotary_tables(n)
            cos, sin = (jnp.cos(freqs), jnp.sin(freqs))
            q = q * cos * scale + rotate_half(q) * sin * scale
            inv = 1.0 / scale
            k = k * cos * inv + rotate_half(k) * sin * inv
            out = local_attention(q, k, v)
            out = out.transpose(0, 2, 1, 3).reshape(b, n, INNER)
            return out @ Wo

        def ffn_layer(x, g, bln, W1, b1, W2, b2):
            mu = x.mean(-1, keepdims=True)
            var = ((x - mu) ** 2).mean(-1, keepdims=True)
            xn = (x - mu) / jnp.sqrt(var + 1e-05) * g + bln
            hg = xn @ W1 + b1
            a, gate = jnp.split(hg, 2, -1)
            return a * jax.nn.gelu(gate, approximate=False) @ W2 + b2
        key = jax.random.key(seed)
        ks = jax.random.split(key, 8)
        B, N = (2, 256)
        init = lambda k, shape: jax.random.normal(k, shape, jnp.float32) * 0.02
        return {'x': jax.random.normal(ks[0], (B, N, DIM), jnp.float32), 'Wqkv': init(ks[1], (DEPTH, DIM, 3 * INNER)), 'q_scale': jnp.ones((DEPTH, DIM_HEAD), jnp.float32), 'k_scale': jnp.ones((DEPTH, DIM_HEAD), jnp.float32), 'Wo': init(ks[2], (DEPTH, INNER, DIM)), 'ln_g': jnp.ones((DEPTH, DIM), jnp.float32), 'ln_b': jnp.zeros((DEPTH, DIM), jnp.float32), 'W1': init(ks[3], (DEPTH, DIM, 2 * DIM_INNER)), 'b1': jnp.zeros((DEPTH, 2 * DIM_INNER), jnp.float32), 'W2': init(ks[4], (DEPTH, DIM_INNER, DIM)), 'b2': jnp.zeros((DEPTH, DIM), jnp.float32)}
    _L0_ffn_in = _L0_ffn_setup()
    _d = {'L0_attn_hidden_states': _L0_attn_in['hidden_states'], 'L0_attn_Wq': _L0_attn_in['Wq'], 'L0_attn_bq': _L0_attn_in['bq'], 'L0_attn_Wk': _L0_attn_in['Wk'], 'L0_attn_bk': _L0_attn_in['bk'], 'L0_attn_Wv': _L0_attn_in['Wv'], 'L0_attn_bv': _L0_attn_in['bv'], 'L0_attn_Wo': _L0_attn_in['Wo'], 'L0_attn_bo': _L0_attn_in['bo'], 'L0_attn_rel_W': _L0_attn_in['rel_W'], 'L0_attn_rel_b': _L0_attn_in['rel_b'], 'L0_attn_logical_bias': _L0_attn_in['logical_bias'], 'L0_attn_gate_W': _L0_attn_in['gate_W'], 'L0_attn_gate_b': _L0_attn_in['gate_b'], 'L0_ffn_Wqkv': _L0_ffn_in['Wqkv'], 'L0_ffn_q_scale': _L0_ffn_in['q_scale'], 'L0_ffn_k_scale': _L0_ffn_in['k_scale'], 'L0_ffn_Wo': _L0_ffn_in['Wo'], 'L0_ffn_ln_g': _L0_ffn_in['ln_g'], 'L0_ffn_ln_b': _L0_ffn_in['ln_b'], 'L0_ffn_W1': _L0_ffn_in['W1'], 'L0_ffn_b1': _L0_ffn_in['b1'], 'L0_ffn_W2': _L0_ffn_in['W2'], 'L0_ffn_b2': _L0_ffn_in['b2']}
    _x0 = _d['L0_attn_hidden_states']
    _d['L0_attn_hidden_states'] = jax.random.normal(jax.random.fold_in(jax.random.key(seed), 1), (1, 2048, 128), dtype=_x0.dtype)
    del _x0
    return _d

def reference(L0_attn_hidden_states, L0_attn_Wq, L0_attn_bq, L0_attn_Wk, L0_attn_bk, L0_attn_Wv, L0_attn_bv, L0_attn_Wo, L0_attn_bo, L0_attn_rel_W, L0_attn_rel_b, L0_attn_logical_bias, L0_attn_gate_W, L0_attn_gate_b, L0_ffn_Wqkv, L0_ffn_q_scale, L0_ffn_k_scale, L0_ffn_Wo, L0_ffn_ln_g, L0_ffn_ln_b, L0_ffn_W1, L0_ffn_b1, L0_ffn_W2, L0_ffn_b2):

    def _L0_attn_ref(hidden_states, Wq, bq, Wk, bk, Wv, bv, Wo, bo, rel_W, rel_b, logical_bias, gate_W, gate_b):
        import jax, jax.numpy as jnp
        import numpy as np
        B, S, D, H = (2, 256, 128, 16)
        HD = D // H
        x = hidden_states
        b, s, d = x.shape
        h = gate_W.shape[0]
        hd = d // h
        scale = hd ** 0.5
        q = (x @ Wq.T + bq).reshape(b, s, h, hd)
        k = (x @ Wk.T + bk).reshape(b, s, h, hd)
        v = (x @ Wv.T + bv).reshape(b, s, h, hd)
        attn_scores = jnp.einsum('bihd,bjhd->bhij', q, k) / scale
        li = x @ rel_W[:, :d].T
        lj = x @ rel_W[:, d:].T
        logits = li[:, :, None, :] + lj[:, None, :, :] + rel_b
        relation_probs = jax.nn.softmax(logits, axis=-1)
        bias = jnp.einsum('bijk,hk->bhij', relation_probs, logical_bias)
        gate = jax.nn.sigmoid(x @ gate_W.T + gate_b)
        gate = jnp.transpose(gate, (0, 2, 1))[..., None]
        attn_scores = attn_scores + gate * bias
        attn_weights = jax.nn.softmax(attn_scores, axis=-1)
        out = jnp.einsum('bhij,bjhd->bihd', attn_weights, v).reshape(b, s, d)
        return out @ Wo.T + bo

    def _L0_ffn_ref(x, Wqkv, q_scale, k_scale, Wo, ln_g, ln_b, W1, b1, W2, b2):
        import jax, jax.numpy as jnp
        import numpy as np
        DIM = 128
        DEPTH = 6
        HEADS = 16
        DIM_HEAD = 64
        WINDOW = 32
        INNER = HEADS * DIM_HEAD
        DIM_INNER = int(DIM * 4 * 2 / 3)
        QK_SCALE = 8.0

        def shift_tokens(t):
            a, s = jnp.split(t, 2, -1)
            s = jnp.pad(s, ((0, 0), (1, 0), (0, 0)))[:, :-1]
            return jnp.concatenate([a, s], -1)

        def l2norm(t):
            return t / jnp.maximum(jnp.linalg.norm(t, axis=-1, keepdims=True), 1e-12)

        def rotate_half(x):
            x1, x2 = jnp.split(x, 2, -1)
            return jnp.concatenate([-x2, x1], -1)

        def rotary_tables(n):
            half = jnp.arange(0, DIM_HEAD, 2, dtype=jnp.float32)
            inv_freq = 1.0 / 10000.0 ** (half / DIM_HEAD)
            t = jnp.arange(n, dtype=jnp.float32)
            freqs = t[:, None] * inv_freq[None, :]
            freqs = jnp.concatenate([freqs, freqs], -1)
            base_scale = (half + 0.4 * DIM_HEAD) / (1.4 * DIM_HEAD)
            power = (t - n // 2) / (WINDOW // 2)
            scale = base_scale[None, :] ** power[:, None]
            scale = jnp.concatenate([scale, scale], -1)
            return (freqs, scale)

        def local_attention(q, k, v):
            b, h, n, d = q.shape
            w = WINDOW
            nw = n // w
            bq = q.reshape(b, h, nw, w, d)
            bk = k.reshape(b, h, nw, w, d)
            bv = v.reshape(b, h, nw, w, d)

            def look(t):
                p = jnp.pad(t, ((0, 0), (0, 0), (1, 0), (0, 0), (0, 0)))
                return jnp.concatenate([p[:, :, :nw], p[:, :, 1:]], axis=3)
            bk2, bv2 = (look(bk), look(bv))
            seq = jnp.arange(n).reshape(nw, w)
            seq_p = jnp.pad(seq, ((1, 0), (0, 0)), constant_values=-1)
            jt = jnp.concatenate([seq_p[:nw], seq_p[1:]], axis=1)
            it = seq[:, :, None]
            jb = jt[:, None, :]
            mask = (it < jb) | (it > jb + w) | (jb == -1)
            sim = jnp.einsum('bhwie,bhwje->bhwij', bq, bk2) * QK_SCALE
            sim = jnp.where(mask, -jnp.finfo(sim.dtype).max, sim)
            attn = jax.nn.softmax(sim, -1)
            out = jnp.einsum('bhwij,bhwje->bhwie', attn, bv2)
            return out.reshape(b, h, n, d)

        def attn_layer(x, Wqkv, qs, ksc, Wo):
            b, n, _ = x.shape
            qkv = x @ Wqkv
            q, k, v = jnp.split(qkv, 3, -1)
            sh = lambda t: t.reshape(b, n, HEADS, DIM_HEAD).transpose(0, 2, 1, 3)
            q, k, v = (sh(q), sh(k), sh(v))
            q = l2norm(q) * qs
            k = l2norm(k) * ksc
            freqs, scale = rotary_tables(n)
            cos, sin = (jnp.cos(freqs), jnp.sin(freqs))
            q = q * cos * scale + rotate_half(q) * sin * scale
            inv = 1.0 / scale
            k = k * cos * inv + rotate_half(k) * sin * inv
            out = local_attention(q, k, v)
            out = out.transpose(0, 2, 1, 3).reshape(b, n, INNER)
            return out @ Wo

        def ffn_layer(x, g, bln, W1, b1, W2, b2):
            mu = x.mean(-1, keepdims=True)
            var = ((x - mu) ** 2).mean(-1, keepdims=True)
            xn = (x - mu) / jnp.sqrt(var + 1e-05) * g + bln
            hg = xn @ W1 + b1
            a, gate = jnp.split(hg, 2, -1)
            return a * jax.nn.gelu(gate, approximate=False) @ W2 + b2
        for i in range(DEPTH):
            x = attn_layer(shift_tokens(x), Wqkv[i], q_scale[i], k_scale[i], Wo[i]) + x
            x = ffn_layer(shift_tokens(x), ln_g[i], ln_b[i], W1[i], b1[i], W2[i], b2[i]) + x
        return x
    x = L0_attn_hidden_states
    x = x + _L0_attn_ref(_layernorm(x, axis=-1), L0_attn_Wq, L0_attn_bq, L0_attn_Wk, L0_attn_bk, L0_attn_Wv, L0_attn_bv, L0_attn_Wo, L0_attn_bo, L0_attn_rel_W, L0_attn_rel_b, L0_attn_logical_bias, L0_attn_gate_W, L0_attn_gate_b)
    x = x + _L0_ffn_ref(_layernorm(x, axis=-1), L0_ffn_Wqkv, L0_ffn_q_scale, L0_ffn_k_scale, L0_ffn_Wo, L0_ffn_ln_g, L0_ffn_ln_b, L0_ffn_W1, L0_ffn_b1, L0_ffn_W2, L0_ffn_b2)
    return x

_drawn_inputs = setup_inputs


def setup_inputs(seed=0):
    import zlib

    import numpy as np

    out = dict(_drawn_inputs(seed))
    spreads = {'L0_attn_bq': (0.0, 0.8),
     'L0_attn_bk': (0.0, 2.0),
     'L0_attn_bv': (0.0, 0.371),
     'L0_attn_bo': (0.0, 0.1),
     'L0_attn_rel_b': (0.0, 2.0),
     'L0_attn_gate_b': (0.0, 2.0),
     'L0_ffn_q_scale': (1.0, 0.6),
     'L0_ffn_k_scale': (1.0, 0.6),
     'L0_ffn_ln_g': (1.0, 0.6),
     'L0_ffn_ln_b': (0.0, 0.8),
     'L0_ffn_b1': (0.0, 0.8),
     'L0_ffn_b2': (0.0, 0.1)}
    factors = {'L0_attn_Wq': 8.0,
     'L0_attn_Wk': 8.0,
     'L0_attn_Wv': 8.0,
     'L0_attn_rel_W': 64.0,
     'L0_attn_logical_bias': 64.0,
     'L0_attn_gate_W': 64.0,
     'L0_ffn_W1': 3.627,
     'L0_ffn_W2': 3.573}
    for name, (base, spread) in spreads.items():
        noise = np.random.default_rng([zlib.crc32(name.encode()), seed]).standard_normal(out[name].shape)
        drawn = base * np.exp(spread * noise) if base else spread * noise
        out[name] = jnp.asarray(drawn.astype(out[name].dtype))
    for name, factor in factors.items():
        out[name] = (out[name] * factor).astype(out[name].dtype)
    return out
```

```python
from contextlib import ExitStack

import numpy as np
import concourse.bass as bass
from concourse import mybir

ALU = mybir.AluOpType
ACT = mybir.ActivationFunctionType
F32 = mybir.dt.float32
BF16 = mybir.dt.bfloat16
FP16 = mybir.dt.float16
AX = mybir.AxisListType

P = 128
S = 2048
D = 128
NB = S // P
H, HD = 16, 8
HH = H // 2
G = 16
NG = P // G
CH = 64
NC_ = S // CH
TERMS = ((0, 0), (0, 1), (1, 0), (1, 1), (0, 2), (2, 0))
GUARD_ROW = len(TERMS) * HD
LEAD = 22


LAYERS = 6
NT = LAYERS * NB
LH, LD = 16, 64
PAIRS = LH // 2
INNER = LH * LD
WIN = 32
NW = P // WIN
FF = D * 4 * 2 // 3
QK_SCALE = 8.0
FC = ((0, P), (P, P), (2 * P, FF - 2 * P))
NWL = 15


def take_waits(eng, count):
    eng.sem_inc(count, 1)


def prepare(nc, io, keep):
    with ExitStack() as ctx:
        sb = lambda n, s, d=F32: ctx.enter_context(nc.sbuf_tensor(n, s, d))
        sem = lambda n: ctx.enter_context(nc.semaphore(n))
        x_in, q_parts = keep["x_res"], keep["q_parts"]
        ident, tmask, dmask = keep["ident"], keep["tmask"], keep["dmask"]
        bn = sb("bn", [P, NB, 6])
        mv = sb("mv", [P, NB, 2])
        rstd = sb("rstd", [P, NB])
        half = sb("half", [P, NB])
        xn = sb("xn", [P, NB, D])
        xnT = sb("xnT", [P, S])
        w_nat = sb("w_nat", [P, 4, D])
        wT = sb("wT", [P, 4, D])
        gate_nat = sb("gate_nat", [H, D])
        rel_nat = sb("rel_nat", [3, 2, D])
        smallT = sb("smallT", [P, H + 6])
        bq = sb("bq", [P, 1])
        bk = sb("bk", [P, 1])
        bv_rows = sb("bv_rows", [P, D])
        bo_rows = sb("bo_rows", [P, D])
        gate_b_rows = sb("gate_b_rows", [P, H])
        rel_b_rows = sb("rel_b_rows", [P, 3])
        lb_rows = sb("lb_rows", [P, H, 3])
        w_drel = sb("w_drel", [P, 4])
        w_lj = sb("w_lj", [P, 2, P])
        b_drel = sb("b_drel", [P, 2])
        li_raw = sb("li_raw", [P, NC_, 4])
        d_lb = sb("d_lb", [P, H])
        full = sb("full", [P, S])
        rest = sb("rest", [P, S])
        part = sb("part", [P, 3, S], BF16)
        gate = sb("gate", [P, P, H])
        rep2 = sb("rep2", [P, NC_, 2, CH])
        rep8 = sb("rep8", [P, 2, 32, P // G, G])
        ps = ctx.enter_context(nc.psum_tensor("ps_prep", [P, 8, 512], F32))

        loads = sem("prep_loads")
        mm = sem("prep_mm")
        ev = sem("prep_ev")
        v = sem("prep_v")
        act = sem("prep_act")
        rs = sem("prep_rstd")
        rep = sem("prep_rep")
        pool = sem("prep_pool")
        stored = sem("prep_stored")
        XN_READY, DIFF_READY, Q_SPLIT, K_SPLIT, GATE_X = "xn", "diff", "q", "k", "g"
        marks = {}

        block = ctx.enter_context(nc.Block())

        @block.vector
        def _(dve):
            n = [0]

            def link(ins):
                n[0] += 1
                ins.then_inc(v, 1)
                dve.wait_ge(v, n[0])

            dve.wait_ge(loads, 16 * LOADS)
            for b in range(NB):
                last = dve.bn_stats(bn[:, b, :], x_in[:, b, :])
            link(last)
            for b in range(NB):
                last = dve.bn_aggr(mv[:, b, :], bn[:, b, :])
            link(last)
            marks["var"] = n[0]
            dve.wait_ge(rs, 1)
            link(dve.tensor_tensor(xn[:], x_in[:], mv[:, :, 0:1].broadcast_to([P, NB, D]), ALU.subtract))
            link(dve.tensor_tensor(xn[:], xn[:], rstd[:].unsqueeze(2).broadcast_to([P, NB, D]), ALU.mult))
            marks[XN_READY] = n[0]
            link(dve.tensor_tensor(x_in[:], x_in[:], bo_rows[:].unsqueeze(1).broadcast_to([P, NB, D]), ALU.add))

            group = [0]

            def bank():
                group[0] += 1
                dve.wait_ge(mm, group[0])
                return ps[:, (group[0] - 1) % 8, :]

            dve.tensor_copy(wT[:].rearrange("p a b -> p (a b)"), bank()).then_inc(ev, 1)
            dve.tensor_copy(smallT[:], bank()[:, 0:H + 6]).then_inc(ev, 1)
            for c in range(4):
                dve.tensor_copy(xnT[:, 512 * c:512 * (c + 1)], bank()).then_inc(ev, 1)
            dve.wait_ge(ev, group[0])
            for half in range(2):
                o = H + 3 * half
                for c, (a, b) in enumerate(((1, 0), (0, 1), (2, 0), (2, 1))):
                    wa, wb = smallT[:, o + a:o + a + 1], smallT[:, o + b:o + b + 1]
                    if half == 0:
                        last = dve.tensor_tensor(w_drel[:, c:c + 1], wa, wb, ALU.subtract)
                    else:
                        k = c % 2
                        last = dve.tensor_tensor(w_lj[:, c // 2, CH * k:CH * (k + 1)], wa.broadcast_to([P, CH]),
                                                 wb.broadcast_to([P, CH]), ALU.subtract)
            link(last)
            marks[DIFF_READY] = n[0]
            for k in range(2):
                r = slice(CH * k, CH * (k + 1))
                dve.tensor_tensor(b_drel[r, 0:1], rel_b_rows[r, 1 - k:2 - k], rel_b_rows[r, k:k + 1], ALU.subtract)
                dve.tensor_tensor(b_drel[r, 1:2], rel_b_rows[r, 2:3], rel_b_rows[r, k:k + 1], ALU.subtract)
                last = dve.tensor_tensor(d_lb[r, :], lb_rows[r, :, k], lb_rows[r, :, 2], ALU.subtract)
            link(last)

            for name, bias, scale in ((Q_SPLIT, bq, HD ** -0.5), (K_SPLIT, bk, 1.0)):
                for c in range(4):
                    dve.tensor_scalar(full[:, 512 * c:512 * (c + 1)], bank(), bias[:, 0:1], scale,
                                      ALU.add, ALU.mult).then_inc(ev, 1)
                dve.wait_ge(ev, group[0])
                if name == K_SPLIT:
                    dve.wait_ge(stored, 16 * 3)
                link(dve.tensor_copy(part[:, 0, :], full[:]))
                link(dve.tensor_tensor(rest[:], full[:], part[:, 0, :], ALU.subtract))
                link(dve.tensor_copy(part[:, 1, :], rest[:]))
                link(dve.tensor_tensor(part[:, 2, :], rest[:], part[:, 1, :], ALU.subtract))
                marks[name] = n[0]
            for c in range(4):
                dve.tensor_tensor(keep["v9"][:, 4 * c:4 * (c + 1), :, 0:HD],
                                  bank().rearrange("p (b h d) -> p b h d", b=4, h=H),
                                  bv_rows[:].rearrange("p (h d) -> p h d", h=H).unsqueeze(1).broadcast_to([P, 4, H, HD]),
                                  ALU.add).then_inc(ev, 1)
            dve.memset(keep["v9"][:, :, :, HD:HD + 1], 1.0)
            for m in range(2):
                for c in range(4):
                    dve.tensor_copy(keep["lj"][:, m, 512 * c:512 * (c + 1)], bank()).then_inc(ev, 1)
            dve.tensor_copy(li_raw[:].rearrange("p c f -> p (c f)"), bank()[:, 0:4 * NC_]).then_inc(ev, 1)
            dve.wait_ge(ev, group[0])
            for k in range(2):
                r = slice(CH * k, CH * (k + 1))
                for m in range(2):
                    dve.tensor_scalar(keep["li"][r, m, :], li_raw[r, :, 2 * m + k], b_drel[r, m:m + 1], None, ALU.add)
            for c in range(4):
                dve.tensor_tensor(gate[:, 32 * c:32 * (c + 1), :], bank().rearrange("p (g h) -> p g h", h=H),
                                  gate_b_rows[:].unsqueeze(1).broadcast_to([P, 32, H]), ALU.add).then_inc(ev, 1)
            dve.wait_ge(act, 1)
            link(dve.tensor_scalar(gate[:], gate[:], 1.0, None, ALU.add))
            link(dve.reciprocal(gate[:], gate[:]))
            full3 = full[:].rearrange("p (g h) -> p g h", h=H)
            link(dve.tensor_tensor(full3, gate[:], d_lb[:].unsqueeze(1).broadcast_to([P, P, H]), ALU.mult))
            dve.wait_ge(stored, 16 * 6)
            link(dve.tensor_copy(part[:, 0, :], full[:]))
            link(dve.tensor_tensor(rest[:], full[:], part[:, 0, :], ALU.subtract))
            link(dve.tensor_copy(part[:, 1, :], rest[:]))
            link(dve.tensor_tensor(part[:, 2, :], rest[:], part[:, 1, :], ALU.subtract))
            cc = keep["coef"][:].rearrange("p g h -> p (g h)")
            link(dve.tensor_scalar(cc, part[:, 0, :], tmask[:, 0:1], None, ALU.mult))
            link(dve.scalar_tensor_tensor(cc, part[:, 1, :], tmask[:, 1:2], cc, ALU.mult, ALU.add))
            link(dve.scalar_tensor_tensor(cc, part[:, 2, :], tmask[:, 2:3], cc, ALU.mult, ALU.add))
            link(dve.tensor_copy(keep["woT"][:], wT[:, 3, :]))

        @block.scalar
        def _(sc):
            sc.wait_ge(ev, 6)
            sc.activation(rep2[:], xnT[:].rearrange("p (c i) -> p c i", i=CH).unsqueeze(2)
                          .broadcast_to([P, NC_, 2, CH]), ACT.Copy).then_inc(rep, 1)
            for c in range(4):
                if c >= 2:
                    sc.wait_ge(mm, 27 + c - 1)
                sc.activation(rep8[:, c % 2], xnT[:, 512 * c:512 * (c + 1)]
                              .rearrange("p (g i) -> p g i", i=G).unsqueeze(2)
                              .broadcast_to([P, 32, P // G, G]), ACT.Copy).then_inc(rep, 1)
            sc.wait_ge(ev, 6 + 8 + 4 + 8 + 1 + 4)
            sc.activation(gate[:], gate[:], ACT.Exp, scale=-1.0).then_inc(act, 1)

        @block.tensor
        def _(pe):
            n = [0]

            def bank():
                if n[0] >= 8:
                    pe.wait_ge(ev, n[0] - 7)
                n[0] += 1
                return ps[:, (n[0] - 1) % 8, :]

            pe.wait_ge(loads, 16 * LOADS)
            o = bank()
            for w in range(4):
                last = pe.transpose(o[:, D * w:D * (w + 1)], w_nat[:, w, :], ident[:])
            last.then_inc(mm, 1)
            o = bank()
            pe.transpose(o[:, 0:H], gate_nat[:], ident[0:H, 0:H])
            pe.transpose(o[:, H:H + 3], rel_nat[:, 0, :], ident[0:3, 0:3])
            pe.transpose(o[:, H + 3:H + 6], rel_nat[:, 1, :], ident[0:3, 0:3]).then_inc(mm, 1)
            pe.wait_ge(v, marks[XN_READY])
            for c in range(4):
                o = bank()
                for b in range(4):
                    last = pe.transpose(o[:, P * b:P * (b + 1)], xn[:, 4 * c + b, :], ident[:])
                last.then_inc(mm, 1)
            pe.wait_ge(ev, 6)
            for w in range(2):
                for c in range(4):
                    pe.matmul(bank(), wT[:, w, :], xnT[:, 512 * c:512 * (c + 1)], start=True, stop=True).then_inc(mm, 1)
            for c in range(4):
                o = bank()
                for b in range(4):
                    t = P * (4 * c + b)
                    last = pe.matmul(o[:, D * b:D * (b + 1)], xnT[:, t:t + P], wT[:, 2, :], start=True, stop=True)
                last.then_inc(mm, 1)
            pe.wait_ge(v, marks[DIFF_READY])
            for m in range(2):
                for c in range(4):
                    pe.matmul(bank(), w_lj[:, m, :], xnT[:, 512 * c:512 * (c + 1)], start=True, stop=True).then_inc(mm, 1)
            o = bank()
            pe.wait_ge(rep, 1)
            for c in range(NC_):
                rows = rep2[:, c].rearrange("p k i -> p (k i)")
                last = pe.matmul(o[:, 4 * c:4 * (c + 1)], rows, w_drel[:], start=True, stop=True)
            last.then_inc(mm, 1)
            for c in range(4):
                o = bank()
                pe.wait_ge(rep, 2 + c)
                for g in range(32):
                    rows = rep8[:, c % 2, g].rearrange("p k i -> p (k i)")
                    last = pe.matmul(o[:, H * g:H * (g + 1)], rows, smallT[:, 0:H], start=True, stop=True)
                last.then_inc(mm, 1)

        @block.gpsimd
        def _(g):
            g.wait_ge(v, marks["var"])
            g.tensor_scalar(mv[:, :, 1], mv[:, :, 1], 1e-5, None, ALU.add).then_inc(pool, 1)
            g.memset(half[:], -0.5).then_inc(pool, 1)
            g.wait_ge(pool, 2)
            g.tensor_tensor(rstd[:], mv[:, :, 1], half[:], ALU.pow).then_inc(rs, 1)
            n = 2
            for tile, value in ((keep["kst"][:], 0.0), (keep["kst"][32:64, :, :], 1.0), (keep["kst"][96:128, :, :], 1.0),
                                (keep["zrow"][:], 0.0), (keep["qst"][:], 0.0)):
                g.memset(tile, value).then_inc(pool, 1)
                n += 1
                g.wait_ge(pool, n)

        @block.sync
        def _(sp):
            count = 0
            rows = lambda ap: ap.partition_broadcast(P)
            for dst, src in (
                (x_in[:], io["x"].rearrange("a (b p) d -> p (a b) d", p=P)), (ident[:], io["ident"]),
                (tmask[:], io["tmask"]), (dmask[:], io["dmask"]),
                (w_nat[:, 0, :], io["Wq"]), (w_nat[:, 1, :], io["Wk"]), (w_nat[:, 2, :], io["Wv"]),
                (w_nat[:, 3, :], io["Wo"]), (gate_nat[:], io["gate_W"]),
                (rel_nat[:], io["rel_W"].rearrange("k (a d) -> k a d", a=2)),
                (bq[:], io["bq"].unsqueeze(1)), (bk[:], io["bk"].unsqueeze(1)),
                (bv_rows[:], rows(io["bv"])), (bo_rows[:], rows(io["bo"])),
                (gate_b_rows[:], rows(io["gate_b"])), (rel_b_rows[:], rows(io["rel_b"])),
                (lb_rows[:], rows(io["logical_bias"])),
            ):
                sp.dma_start(dst, src).then_inc(loads, 16)
                count += 1
            assert count == LOADS
            sp.wait_ge(v, marks[Q_SPLIT])
            for a in range(3):
                sp.dma_start(q_parts[a], part[:, a, :]).then_inc(stored, 16)
            sp.wait_ge(v, marks[K_SPLIT])
            for a in range(3):
                sp.dma_start(io["k_parts"][a], part[:, a, :]).then_inc(stored, 16)
            sp.wait_ge(stored, 16 * 6)
            sp.wait_ge(pool, 5)
            for hp in range(2):
                for t, (_, b) in enumerate(TERMS):
                    r = 64 * hp + HD * t
                    src = io["k_parts"][b].rearrange("(pair hp d) s -> hp d pair s", hp=2, d=HD)[hp]
                    sp.dma_start(keep["kst"][r:r + HD, :, :], src).then_inc(stored, 16)
            sp.wait_ge(stored, 16 * 18)


LOADS = 17


def attention(nc, io, keep):
    with ExitStack() as ctx:
        sb = lambda n, s, d=F32: ctx.enter_context(nc.sbuf_tensor(n, s, d))
        sem = lambda n: ctx.enter_context(nc.semaphore(n))
        kst, qst, v9, coef = keep["kst"], keep["qst"], keep["v9"], keep["coef"]
        lj, li, x_res, woT, ident, dmask = keep["lj"], keep["li"], keep["x_res"], keep["woT"], keep["ident"], keep["dmask"]
        zrow = keep["zrow"]
        pst = sb("pst", [P, 2, NG, S], FP16)
        diag = sb("diag", [P, 2, NG, H, G], BF16)
        prob = sb("prob", [P, 2, HH * P])
        colmax = sb("colmax", [P, 2, HH * P])
        rel_exp = sb("rel_exp", [P, 2, 2, 512])
        own = sb("own", [P, 2, 1])
        rel_sum = sb("rel_sum", [P, 2, 512])
        rel_p = sb("rel_p", [P, 2, 512])
        stage = sb("stage", [P, 2, 2, S], FP16)
        rmax = sb("rmax", [P, HH])
        grest = sb("grest", [P, 2, HH])
        gpart = sb("gpart", [P, 3, HH], BF16)
        guard = sb("guard", [P, 2, 3, HH // 2])
        guardT = sb("guardT", [2 * 3 * HH // 2, P], BF16)
        outT = sb("outT", [P, 2, P])
        rden = sb("rden", [P, HH])
        heads = sb("heads", [P, D])
        headsT = sb("headsT", [P, D])
        x1 = sb("x1_sb", [P, D])
        psA = ctx.enter_context(nc.psum_tensor("psA", [P, 2, 512], F32))
        psB = ctx.enter_context(nc.psum_tensor("psB", [P, 2, 2, 512], F32))
        psO = ctx.enter_context(nc.psum_tensor("psO", [P, 512], F32))
        psM = ctx.enter_context(nc.psum_tensor("psM", [P, 512], F32))

        a_done = sem("a_done")
        a_read = sem("a_read")
        b_done = sem("b_done")
        e_done = sem("e_done")
        pv_done = sem("pv_done")
        o_read = sem("o_read")
        m_done = sem("m_done")
        m_read = sem("m_read")
        dch = sem("att_dve_chain")
        guard_in = sem("guard_in")
        guard_dma = sem("guard_dma")
        x1_dma = sem("x1_dma")
        re_done = sem("re_done")
        rc_done = sem("rc_done")
        rs_done = sem("rs_done")
        rr_done = sem("rr_done")
        own_done = sem("own_done")
        r1_done = sem("r1_done")
        rp_done = sem("rp_done")
        rq_done = sem("rq_done")
        pst_dma = [sem(f"pst_dma{i}") for i in range(4)]
        p_dma = [sem(f"p_dma{i}") for i in range(2)]
        p_parts = io["p_parts"]
        q_dma = [sem(f"q_dma{i}") for i in range(2)]
        diag_done = sem("diag_done")
        zero_o = sem("zero_o")
        pool_waits = sem("pool_waits")
        sp_waits = sem("sp_waits")
        QD = 2 * len(TERMS) + 2
        PD = 2 * 4

        def unit_events(ul, first, last):
            ev = {}
            if not (first and ul == 0):
                ev[2] = "out"
                if ul % 2 == 0:
                    ev[4], ev[6] = "heads", "proj"
            if not (last and ul == 3):
                ev[10], ev[11], ev[13] = "max0", "max1", "guard"
            return ev

        def events_before(it, ul, step, first, last):
            n = 3 if first else 20 * it
            for w in range(ul + 1):
                e = unit_events(w, first, last)
                n = n + sum(1 for k in e if w < ul or k < step)
            return n

        block = ctx.enter_context(nc.Block())

        @block.tensor
        def _(pe):
            def scores(dst, par, half, jb):
                for hl in range(HH):
                    h = HH * half + hl
                    pe.matmul(dst[:, hl // 4, P * (hl % 4):P * (hl % 4 + 1)], kst[:, h // 2, P * jb:P * (jb + 1)],
                              qst[:, par, h, :], start=(hl % 4 == 0), stop=False, skip_group_check=True)
                for g in range(NG):
                    for q in range(2):
                        o = dst[:, q, :].rearrange("p (h i) -> p h i", h=4)[:, :, G * g:G * (g + 1)]
                        h0 = HH * half + 4 * q
                        last = pe.matmul(o, pst[:, par, g, P * jb:P * (jb + 1)], diag[:, par, g, h0:h0 + 4, :],
                                         start=False, stop=(g == NG - 1), skip_group_check=True)
                return last

            def a_tile(a, ul, jb, block_no):
                pe.wait_ge(a_read, a) if not (isinstance(a, int) and a == 0) else None
                if ul % 2 == 0 and jb == 0:
                    par = (ul // 2) % 2
                    for c in range(2):
                        pe.wait_ge(pst_dma[2 * par + c], block_times(block_no) * 16 * PD)
                    pe.wait_ge(q_dma[par], block_times(block_no) * 16 * QD)
                    pe.wait_ge(diag_done, block_no + 1)
                scores(psA, (ul // 2) % 2, ul % 2, jb).then_inc(a_done, 1)

            def block_times(n):
                return n // 2 + 1

            def values(b, jb, half, first_unit_wait):
                pe.wait_ge(e_done, b + 1)
                if jb == 0 and not (isinstance(first_unit_wait, int) and first_unit_wait == 0):
                    pe.wait_ge(o_read, first_unit_wait)
                for hl in range(HH):
                    s, c = hl // 4, hl % 4
                    last = pe.matmul(psO[32 * c:32 * c + HD + 1, P * s:P * (s + 1)], v9[:, jb, HH * half + hl, :],
                                     prob[:, jb % 2, P * hl:P * (hl + 1)], start=(jb == 0 and s == 0),
                                     stop=(jb == NB - 1), skip_group_check=True)
                last.then_inc(pv_done, 1)

            def through_m(kind, n, unit, ul):
                pe.wait_ge(m_read, n) if not (isinstance(n, int) and n == 0) else None
                if kind in ("max0", "max1"):
                    u = 1 if kind == "max1" else 0
                    par = (ul + 1) % 2
                    pe.wait_ge(a_read, NB * (unit + 2))
                    for k in range(4):
                        c = P * (4 * u + k)
                        last = pe.transpose(psM[:, P * k:P * (k + 1)], colmax[:, par, c:c + P], ident[:])
                elif kind == "guard":
                    pe.wait_ge(guard_in, unit + 2)
                    last = pe.transpose(psM[0:3 * HH, 0:P], guard[:].rearrange("p a b c -> p (a b c)"), ident[:])
                elif kind == "out":
                    pe.wait_ge(o_read, unit)
                    for s in range(2):
                        last = pe.transpose(psM[:, P * s:P * (s + 1)], outT[:, s, :], ident[:])
                elif kind == "heads":
                    last = pe.transpose(psM[:, 0:P], heads[:], ident[:])
                else:
                    last = pe.matmul(psM[:, 0:D], headsT[:], woT[:], start=True, stop=True)
                last.then_inc(m_done, 1)

            def body(it, first=False, last=False):
                for st in range(4 * NB):
                    ul, jb = divmod(st, NB)
                    b = it * (4 * NB) + st
                    if not (last and st + LEAD >= 4 * NB):
                        al, ja = divmod(st + LEAD, NB)
                        a_tile(b + LEAD, al, ja, it * 2 + al // 2)
                    if not (first and st < 2):
                        pe.wait_ge(e_done, b - 1)
                    if jb == 0:
                        pe.wait_ge(guard_dma, (it * 4 + ul + 1) * 16 * 6)
                    scores(psB[:, st % 2], (ul // 2) % 2, ul % 2, jb).then_inc(b_done, 1)
                    if not (first and st == 0):
                        pu, pj = divmod(st - 1, NB)
                        values(b - 1, pj, pu % 2, it * 4 + pu)
                    e = unit_events(ul, first, last)
                    if jb in e:
                        through_m(e[jb], events_before(it, ul, jb, first, last), it * 4 + ul, ul)

            pe.wait_ge(zero_o, 1)
            for a in range(LEAD):
                ul, ja = divmod(a, NB)
                a_tile(a, ul, ja, 0)
                if a == 17:
                    through_m("max0", 0, -1, -1)
                if a == 18:
                    through_m("max1", 1, -1, -1)
                if a == 20:
                    through_m("guard", 2, -1, -1)
            body(0, first=True)
            with pe.Fori(1, 7) as it:
                body(it)
            body(7, last=True)
            values(8 * 4 * NB - 1, NB - 1, 1, 0)
            n = 20 * 7 + 20 - 3
            through_m("out", n, 32, 0)
            through_m("heads", n + 1, 32, 0)
            through_m("proj", n + 2, 32, 0)

        @block.scalar
        def _(act):
            def exp_tile(b, st, first):
                act.wait_ge(b_done, b + 1)
                if not (first and st < 2):
                    act.wait_ge(pv_done, b - 1)
                act.activation(prob[:, st % 2, :], psB[:, st % 2].rearrange("p a b -> p (a b)"), ACT.Exp)\
                   .then_inc(e_done, 1)

            def rel(n, q):
                act.wait_ge(rc_done, n + 1)
                e = rel_exp[:, q % 2].rearrange("p m j -> p (m j)")
                act.activation(e, e, ACT.Exp).then_inc(re_done, 1)

            def first_part(n, c, cm, q):
                act.wait_ge(rr_done, n + 1)
                if q == 0 and not (isinstance(c, int) and c < 2):
                    act.wait_ge(p_dma[cm % 2], c // 2 * 16)
                act.activation(stage[:, cm % 2, 0, 512 * q:512 * (q + 1)], rel_p[:, q % 2, :], ACT.Copy).then_inc(rp_done, 1)

            def body(it, first=False, last=False):
                for st in range(4 * NB):
                    ul, jb = divmod(st, NB)
                    exp_tile(it * (4 * NB) + st, st, first)
                    if not last and jb in (1, 3, 5, 7):
                        rel(((it * 2 + ul // 2 + 2) * 2 + ul % 2) * 4 + jb // 2, jb // 2)
                    if not last and jb in (4, 6, 8, 10):
                        c = (it * 2 + ul // 2 + 2) * 2 + ul % 2
                        first_part(c * 4 + jb // 2 - 2, c, ul, jb // 2 - 2)

            for c in range(4):
                rel(4 * c, 0)
                for q in range(4):
                    if q < 3:
                        rel(4 * c + q + 1, q + 1)
                    first_part(4 * c + q, c, c, q)
            body(0, first=True)
            with act.Fori(1, 7) as it:
                body(it)
            body(7, last=True)

        @block.gpsimd
        def _(pool):
            def quarter_args(c, n, q):
                if not (isinstance(n, int) and n < 2):
                    pool.wait_ge(rs_done, n - 1)
                if q == 0:
                    pool.tensor_copy(own[:], li[:, :, c:c + 1] if isinstance(c, int) else li[:, :, bass.ds(c, 1)])\
                        .then_inc(own_done, 1)
                    pool.wait_ge(own_done, c + 1)
                take_waits(pool, pool_waits)
                for m in range(2):
                    last = pool.tensor_scalar(rel_exp[:, q % 2, m, :], lj[:, m, 512 * q:512 * (q + 1)], own[:, m, :],
                                              80.0, ALU.add, ALU.min)
                last.then_inc(rc_done, 1)

            def quarter_sum(n, q):
                pool.wait_ge(re_done, n + 1)
                if not (isinstance(n, int) and n < 2):
                    pool.wait_ge(rr_done, n - 1)
                pool.tensor_tensor(rel_sum[:, q % 2, :], rel_exp[:, q % 2, 0, :], rel_exp[:, q % 2, 1, :],
                                   ALU.add).then_inc(rs_done, 1)

            def quarter_rest(n, q, half):
                pool.wait_ge(rp_done, n + 1)
                pool.tensor_tensor(stage[:, half, 1, 512 * q:512 * (q + 1)], rel_p[:, q % 2, :],
                                   stage[:, half, 0, 512 * q:512 * (q + 1)], ALU.subtract).then_inc(rq_done, 1)

            def chunk(c, cm, staged):
                if staged:
                    pool.wait_ge(p_dma[cm % 2], c // 2 * 16)
                quarter_args(c, c * 4, 0)
                for q in range(4):
                    if q < 3:
                        quarter_args(c, c * 4 + q + 1, q + 1)
                    quarter_sum(c * 4 + q, q)
                    if q > 0:
                        quarter_rest(c * 4 + q - 1, q - 1, cm % 2)
                quarter_rest(c * 4 + 3, 3, cm % 2)

            def diagonal(block_no, par):
                g0 = block_no * NG
                src = coef[:, g0:g0 + NG, :] if isinstance(g0, int) else coef[:, bass.ds(g0, NG), :]
                pool.tensor_tensor(diag[:, par].rearrange("p g h i -> p (g h) i"),
                                   src.rearrange("p g h -> p (g h)").unsqueeze(2).broadcast_to([P, NG * H, G]),
                                   dmask[:].unsqueeze(1).broadcast_to([P, NG * H, G]), ALU.mult).then_inc(diag_done, 1)

            def body(it, first=False, last=False):
                for ul in range(4):
                    blk = it * 2 + ul // 2
                    if ul % 2 == 0 and not (first and ul == 0) and not (last and ul == 2):
                        pool.wait_ge(b_done, blk * (2 * NB))
                        diagonal(blk + 1, (ul // 2 + 1) % 2)
                    if not last:
                        chunk((blk + 2) * 2 + ul % 2, ul, True)

            for c in range(4):
                chunk(c, c, c >= 2)
            diagonal(0, 0)
            diagonal(1, 1)
            body(0, first=True)
            with pool.Fori(1, 7) as it:
                body(it)
            body(7, last=True)

        @block.vector
        def _(dve):
            k = [0]

            def a_max(a, ul, ja):
                dve.wait_ge(a_done, a + 1)
                src, dst = psA[:].rearrange("p a b -> p (a b)"), colmax[:, ul % 2, :]
                if ja == 0:
                    dve.tensor_copy(dst, src).then_inc(a_read, 1)
                else:
                    dve.wait_ge(a_read, a)
                    dve.tensor_tensor(dst, src, dst, ALU.max).then_inc(a_read, 1)

            def recip(n, q):
                dve.wait_ge(rs_done, n + 1)
                if not (isinstance(n, int) and n < 2):
                    dve.wait_ge(rq_done, n - 1)
                dve.tensor_scalar(rel_sum[:, q % 2, :], rel_sum[:, q % 2, :], 1.0, None, ALU.add).then_inc(r1_done, 1)
                dve.wait_ge(r1_done, n + 1)
                dve.reciprocal(rel_p[:, q % 2, :], rel_sum[:, q % 2, :]).then_inc(rr_done, 1)

            def read_m(kind, n, unit, chain):
                def link(ins):
                    chain[0] = chain[0] + 1
                    ins.then_inc(dch, 1)
                    dve.wait_ge(dch, chain[0])

                dve.wait_ge(m_done, n + 1)
                if kind in ("max0", "max1"):
                    u = 1 if kind == "max1" else 0
                    dve.tensor_reduce(rmax[:, 4 * u:4 * u + 4], psM[:].rearrange("p (h j) -> p h j", h=4), AX.X,
                                      ALU.max).then_inc(m_read, 1)
                    if u:
                        dve.wait_ge(m_read, n + 1)
                        link(dve.tensor_scalar(grest[:, 0, :], rmax[:], -1.0, None, ALU.mult))
                        link(dve.tensor_copy(gpart[:, 0, :], grest[:, 0, :]))
                        link(dve.tensor_tensor(grest[:, 1, :], grest[:, 0, :], gpart[:, 0, :], ALU.subtract))
                        link(dve.tensor_copy(gpart[:, 1, :], grest[:, 1, :]))
                        link(dve.tensor_tensor(gpart[:, 2, :], grest[:, 1, :], gpart[:, 1, :], ALU.subtract))
                        dve.tensor_copy(guard[:].rearrange("p hp a pair -> p a pair hp"),
                                        gpart[:].rearrange("p a (pair hp) -> p a pair hp", hp=2)).then_inc(guard_in, 1)
                elif kind == "guard":
                    if not (isinstance(unit, int) and unit < 0):
                        dve.wait_ge(guard_dma, (unit + 1) * 16 * 6)
                    dve.tensor_copy(guardT[:], psM[0:3 * HH, 0:P]).then_inc(m_read, 1)
                elif kind == "out":
                    o = psM[:, 0:2 * P].rearrange("p (h r) -> p h r", r=32)
                    link(dve.reciprocal(rden[:], o[:, :, HD]))
                    half = read_m.half
                    dve.tensor_tensor(heads[:, D // 2 * half:D // 2 * (half + 1)].rearrange("p (h d) -> p h d", d=HD),
                                      o[:, :, 0:HD], rden[:].unsqueeze(2).broadcast_to([P, HH, HD]), ALU.mult)\
                        .then_inc(m_read, 1)
                elif kind == "heads":
                    dve.tensor_copy(headsT[:], psM[:, 0:P]).then_inc(m_read, 1)
                else:
                    blk = (unit - 1) // 2
                    xr = x_res[:, blk, :] if isinstance(blk, int) else x_res[:, bass.ds(blk, 1), :].rearrange("p a d -> p (a d)")
                    if not (isinstance(blk, int) and blk == 0):
                        dve.wait_ge(x1_dma, blk * 16)
                    dve.tensor_tensor(x1[:], psM[:, 0:D], xr, ALU.add).then_inc(m_read, 1)

            def chain_before(it, ul, step, first, last):
                n = 5 if first else it * 24 + 4
                for w in range(ul + 1):
                    for s_, kd in unit_events(w, first, last).items():
                        if w < ul or s_ < step:
                            n = n + {"max1": 5, "out": 1}.get(kd, 0)
                return n

            def take(e, step, it, ul, first, last):
                if step in e:
                    read_m.half = (ul + 1) % 2
                    read_m(e[step], events_before(it, ul, step, first, last), it * 4 + ul,
                           [chain_before(it, ul, step, first, last)])

            def body(it, first=False, last=False):
                for st in range(4 * NB):
                    ul, jb = divmod(st, NB)
                    b = it * (4 * NB) + st
                    if jb == 1 and not (first and ul == 0):
                        dve.wait_ge(pv_done, b - 1)
                        dve.tensor_copy(outT[:].rearrange("p a b -> p (a b)"), psO[:, 0:2 * P]).then_inc(o_read, 1)
                    if not (last and st + LEAD >= 4 * NB):
                        al, ja = divmod(st + LEAD, NB)
                        a_max(b + LEAD, al, ja)
                    if jb > 0:
                        take(unit_events(ul, first, last), jb - 1, it, ul, first, last)
                    if not last and jb in (3, 5, 7, 9):
                        q = (jb - 3) // 2
                        recip(((it * 2 + ul // 2 + 2) * 2 + ul % 2) * 4 + q, q)

            dve.memset(psO[:], 0.0).then_inc(zero_o, 1)
            for n in range(16):
                recip(n, n % 4)
            for a in range(LEAD):
                ul, ja = divmod(a, NB)
                a_max(a, ul, ja)
                if a == 18:
                    read_m("max0", 0, -1, [0])
                if a == 19:
                    read_m("max1", 1, -1, [0])
                if a == 21:
                    read_m("guard", 2, -1, [5])
            body(0, first=True)
            with dve.Fori(1, 7) as it:
                body(it)
            body(7, last=True)
            dve.wait_ge(pv_done, 8 * 4 * NB)
            dve.tensor_copy(outT[:].rearrange("p a b -> p (a b)"), psO[:, 0:2 * P]).then_inc(o_read, 1)
            n = 20 * 7 + 20 - 3
            read_m.half = 1
            read_m("out", n, 32, [chain_before(7, 3, NB, False, True)])
            read_m("heads", n + 1, 32, [0])
            read_m("proj", n + 2, 32, [0])

        @block.sync
        def _(sp):
            def queries(block_no, par):
                t0 = block_no * P
                for hp in range(2):
                    for t, (a, _) in enumerate(TERMS):
                        r = 64 * hp + HD * t
                        src = keep["q_parts"][a].rearrange("(pair hp d) s -> hp d pair s", hp=2, d=HD)[hp]
                        src = src[:, :, t0:t0 + P] if isinstance(t0, int) else src[:, :, bass.ds(t0, P)]
                        sp.dma_start(qst[r:r + HD, par, hp::2, :], src).then_inc(q_dma[par], 16)
                    r = 64 * hp + GUARD_ROW
                    sp.dma_start(qst[r:r + 3, par, hp::2, :], zrow[:]).then_inc(q_dma[par], 16)

            def chunk_out(c, cm):
                sp.wait_ge(rq_done, c * 4 + 4)
                take_waits(sp, sp_waits)
                if isinstance(c, int):
                    there = p_parts[c]
                else:
                    there = p_parts[bass.ds(c, 1)].rearrange("a t p j -> (a t) p j")
                sp.dma_start(there.rearrange("t p j -> p t j"), stage[:, cm % 2]).then_inc(p_dma[cm % 2], 16)

            def chunk_in(c, cm, par):
                sp.wait_ge(p_dma[cm % 2], c // 2 * 16 + 16)
                take_waits(sp, sp_waits)
                for k in range(2):
                    for t in range(4):
                        if isinstance(c, int):
                            there = p_parts[c, 1 if t == 3 else 0]
                        else:
                            there = p_parts[bass.ds(c, 1), 1 if t == 3 else 0].rearrange("a p j -> (a p) j")
                        w = CH * k + G * t
                        sp.dma_start(pst[w:w + G, par, 4 * (cm % 2):4 * (cm % 2) + 4, :],
                                     there[CH * k:CH * (k + 1), :].rearrange("(g i) j -> i g j", i=G)).then_inc(pst_dma[cm], 16)

            def guards(read, ul):
                sp.wait_ge(m_read, read)
                par, half = (ul // 2) % 2, ul % 2
                for hp in range(2):
                    for a in range(3):
                        r = 4 * (3 * hp + a)
                        h0 = HH * half + hp
                        dst = qst[64 * hp + GUARD_ROW + a:64 * hp + GUARD_ROW + a + 1, par, h0:h0 + HH - 1:2, :]
                        sp.dma_start(dst, guardT[r:r + 4, :]).then_inc(guard_dma, 16)

            def body(it, first=False, last=False):
                for ul in range(4):
                    blk = it * 2 + ul // 2
                    if ul % 2 == 0 and not (first and ul == 0) and not (last and ul == 2):
                        sp.wait_ge(b_done, blk * (2 * NB))
                        take_waits(sp, sp_waits)
                        queries(blk + 1, (ul // 2 + 1) % 2)
                        for c in range(2):
                            chunk_in((blk + 1) * 2 + c, (ul + 2 + c) % 4, (ul // 2 + 1) % 2)
                    if ul % 2 == 0 and not (first and ul == 0):
                        store(blk - 1, events_before(it, ul, 6, first, last) + 1)
                    if not last:
                        chunk_out((blk + 2) * 2 + ul % 2, ul)
                    if not (last and ul == 3):
                        guards(events_before(it, ul, 13, first, last) + 1, (ul + 1) % 4)

            def store(blk, read):
                sp.wait_ge(m_read, read)
                take_waits(sp, sp_waits)
                dst = io["x1"].rearrange("(b p) d -> p b d", p=P)
                dst = dst[:, blk, :] if isinstance(blk, int) else dst[:, bass.ds(blk, 1), :].rearrange("p a d -> p (a d)")
                sp.dma_start(dst, x1[:]).then_inc(x1_dma, 16)

            queries(0, 0)
            queries(1, 1)
            for c in range(4):
                chunk_out(c, c)
                chunk_in(c, c, c // 2)
            guards(3, 0)
            body(0, first=True)
            with sp.Fori(1, 7) as it:
                body(it)
            body(7, last=True)
            store(NB - 1, 20 * 7 + 20 - 3 + 3)
            sp.wait_ge(x1_dma, 16 * NB)


def global_attention(nc, ctx, io):
    sb = lambda n, s, d=F32: ctx.enter_context(nc.sbuf_tensor(n, s, d))
    keep = {
        "x_res": sb("x_res", [P, NB, D]), "ident": sb("ident", [P, P]), "tmask": sb("tmask", [P, 3]),
        "dmask": sb("dmask", [P, G]), "kst": sb("kst", [P, H // 2, S], BF16), "qst": sb("qst", [P, 2, H, P], BF16),
        "v9": sb("v9", [P, NB, H, HD + 1]), "coef": sb("coef", [P, P, H], BF16), "lj": sb("lj", [P, 2, S]),
        "li": sb("li", [P, 2, NC_]), "woT": sb("woT", [P, D]), "zrow": sb("zrow", [3, H // 2, P], BF16),
        "q_parts": io["q_parts"],
    }
    prepare(nc, io, keep)
    attention(nc, io, keep)


def wait(eng, sem, value):
    if not (isinstance(value, int) and value <= 0):
        eng.wait_ge(sem, value)


def at(ap, dim1):
    if isinstance(dim1, int):
        return ap[:, dim1]
    names = "abcdef"[:len(ap.shape) - 2]
    one = ap[:, bass.ds(dim1, 1)]
    free = " ".join(names)
    return one.rearrange(f"p o {free} -> p (o {names[0]}) {' '.join(names[1:])}")


def local_layers(nc, io):
    with ExitStack() as ctx:
        sb = lambda n, s, d=F32: ctx.enter_context(nc.sbuf_tensor(n, s, d))
        sem = lambda n: ctx.enter_context(nc.semaphore(n))
        wqkv = sb("wqkv", [P, 2, 3 * INNER])
        wo = sb("wo", [P, 2, PAIRS * D])
        w1 = sb("w1", [P, 2, 2 * FF])
        w2 = sb("w2", [P, 2, 3 * D])
        b1_rows = sb("b1_rows", [P, 2, 2 * FF])
        b2_rows = sb("b2_rows", [P, 2, D])
        ln_cols = sb("ln_cols", [P, 2, 2])
        scale_rows = sb("scale_rows", [P, 2, 4 * LD])
        xa = sb("xa", [P, NB + 1, D])
        xm = sb("xm", [P, NB + 1, D])
        rope = sb("rope", [P, NB, 4 * LD])
        mask32 = sb("mask32", [P, 2, 2 * WIN])
        mask = sb("mask", [P, NB, 2 * WIN], BF16)
        ident = sb("ident2", [P, P])
        identb = sb("identb", [P, P], BF16)
        xs_a = sb("xs_a", [P, 2, D])
        xs_f = sb("xs_f", [P, D])
        xsT = sb("xsT", [P, 2, P])
        tab = sb("tab", [P, 2, 4, LD])
        sq = sb("sq", [P, 2, INNER])
        t1 = sb("t1", [P, 2, INNER])
        t2 = sb("t2", [P, 2, INNER])
        ssq = sb("ssq", [P, 2, LH])
        rnorm = sb("rnorm", [P, 2, LH])
        qk = sb("qk", [P, 2, INNER])
        qT = sb("qT", [P, PAIRS, P])
        kT = sb("kT", [P, 2, PAIRS, WIN + P])
        vs = sb("vs", [P, 2, INNER])
        v2 = sb("v2", [P, NW, 2, PAIRS, LD])
        mx = sb("mx", [P, 2, PAIRS])
        pr = sb("pr", [P, PAIRS, 2, 2 * WIN])
        den = sb("den", [P, LH])
        rden = sb("rden2", [P, LH])
        prT = sb("prT", [P, PAIRS, P])
        ot = sb("ot", [P, INNER])
        otT = sb("otT", [P, PAIRS, P])
        bn = sb("bn2", [P, 6])
        mv = sb("mv2", [P, 2])
        var = sb("var", [P, 1])
        rstd = sb("rstd2", [P, 1])
        half1 = sb("half1", [P, 2 * LH])
        has_prev = sb("has_prev", [P, NB])
        xn = sb("xn2", [P, D])
        xnT = sb("xnT2", [P, P])
        hs = sb("hs", [P, 2, FF])
        gs = sb("gs", [P, FF])
        gT = sb("gT", [P, 3, P])
        xmb = sb("xmb", [P, D])
        bn16 = sb("bn16", [P, NB, 6])
        mv16 = sb("mv16", [P, NB, 2])
        rs16 = sb("rs16", [P, NB])
        R = [ctx.enter_context(nc.psum_tensor(f"R{i}", [P, 2, 512], F32)) for i in range(4)]
        flat = [r[:].rearrange("p a b -> p (a b)") for r in R]

        names = """init_dma init_dve init_pool init_act w_dma xs_f_dma v2_dma xT_done xT_ready q_done k_done v_done sq_done
            tq_done tk_done ssq_done clamp_done rn_done add_done qk_done qT_done kT_done qT_ready kT_ready kprev_done
            s_done mx_done sub_done exp_done sum_done rden_done pT_done pT_ready pv2_done o_ready oT_done oT_ready
            wo_done x2_done st_done lnv_done eps_done rstd_done xn_done xnT_done xnT_ready h_done hb_done gelu_done
            g_done gT_done gT_ready w2_done xmb_done x3_done v_ready tab_done out_dma pool_taken dve_taken sp_taken""".split()
        m = {n: sem(n) for n in names}
        xs_a_dma = [sem("xs_a_dma0"), sem("xs_a_dma1")]

        with nc.Block() as block:
            @block.sync
            def _(sp):
                for dst, src in ((xm[:, 1:NB + 1, :], io["x1"].rearrange("(b p) d -> p b d", p=P)),
                                 (rope[:], io["rope"]), (mask32[:], io["mask"]), (ident[:], io["ident"])):
                    sp.dma_start(dst, src).then_inc(m["init_dma"], 16)

            @block.gpsimd
            def _(pool):
                n = 0
                for tile, value in ((half1[:], -0.5), (vs[:], 0.0), (v2[:], 0.0), (kT[:], 0.0)):
                    pool.memset(tile, value).then_inc(m["init_pool"], 1)
                    n += 1
                pool.wait_ge(m["init_dve"], 2)
                pool.wait_ge(m["init_pool"], n)
                pool.tensor_scalar(mv16[:, :, 1], mv16[:, :, 1], 1e-5, None, ALU.add).then_inc(m["init_pool"], 1)
                pool.wait_ge(m["init_pool"], n + 1)
                pool.tensor_tensor(rs16[:], mv16[:, :, 1], half1[:, 0:NB], ALU.pow).then_inc(m["init_pool"], 1)

            @block.vector
            def _(dve):
                dve.wait_ge(m["init_dma"], 16 * 4)
                for b in range(NB):
                    last = dve.bn_stats(bn16[:, b, :], xm[:, b + 1, :])
                last.then_inc(m["init_dve"], 1)
                dve.wait_ge(m["init_dve"], 1)
                for b in range(NB):
                    last = dve.bn_aggr(mv16[:, b, :], bn16[:, b, :])
                last.then_inc(m["init_dve"], 1)
                dve.memset(xa[:, 0, :], 0.0)
                dve.memset(xm[:, 0, :], 0.0)
                dve.memset(has_prev[:, 0:1], 0.0)
                dve.memset(has_prev[:, 1:NB], 1.0)
                dve.tensor_copy(identb[:], ident[:])
                dve.tensor_copy(mask[:, 0, :], mask32[:, 0, :])
                dve.tensor_copy(mask[:, 1:NB, :], mask32[:, 1:2, :].broadcast_to([P, NB - 1, 2 * WIN]))
                dve.wait_ge(m["init_pool"], 6)
                dve.tensor_tensor(xa[:, 1:NB + 1, :], xm[:, 1:NB + 1, :], mv16[:, :, 0:1].broadcast_to([P, NB, D]),
                                  ALU.subtract).then_inc(m["init_dve"], 1)
                dve.wait_ge(m["init_dve"], 3)
                dve.tensor_tensor(xa[:, 1:NB + 1, :], xa[:, 1:NB + 1, :], rs16[:].unsqueeze(2).broadcast_to([P, NB, D]),
                                  ALU.mult).then_inc(m["x3_done"], NB)

        def wp(n):
            return (n // NB) % 2

        def steps(eng, step):
            for s in range(4):
                step(s, s % 2)
            with eng.Fori(2, NT // 2 - 1) as i:
                step(i * 2, 0)
                step(i * 2 + 1, 1)
            for s in range(NT - 2, NT + 2):
                step(s, s % 2)

        def stages(s):
            if isinstance(s, int):
                return s < NT, 1 <= s <= NT, 2 <= s
            return True, True, True

        with nc.Block() as block:
            @block.tensor
            def _(pe):
                def turn_x(n, par):
                    wait(pe, xs_a_dma[par], (n // 2 + 1) * 48)
                    wait(pe, m["x3_done"], n - 2 + NB)
                    wait(pe, m["tq_done"], n)
                    pe.transpose(flat[0][:, 0:P], xs_a[:, par, :], ident[:]).then_inc(m["xT_done"], 1)

                def project(n, par, which, bank, done):
                    w = at(wqkv, wp(n))
                    for c in range(2):
                        last = pe.matmul(R[bank][:, c, :], xsT[:, par, :],
                                         w[:, INNER * which + 512 * c:INNER * which + 512 * (c + 1)], start=True, stop=True)
                    last.then_inc(m[done], 1)

                def step(s, par):
                    a, b, c = stages(s)
                    n, k = s - 1, s - 2
                    if b:
                        wait(pe, m["qk_done"], 2 * n + 1)
                        wait(pe, m["oT_ready"], n)
                        wait(pe, m["tk_done"], n + 1)
                        for i in range(PAIRS):
                            last = pe.transpose(flat[1][:, P * i:P * (i + 1)], qk[:, 0, P * i:P * (i + 1)], ident[:])
                        last.then_inc(m["qT_done"], 1)
                        wait(pe, m["qk_done"], 2 * n + 2)
                        wait(pe, m["x2_done"], n)
                        wait(pe, m["v_ready"], n + 1)
                        for i in range(PAIRS):
                            last = pe.transpose(flat[2][:, P * i:P * (i + 1)], qk[:, 1, P * i:P * (i + 1)], ident[:])
                        last.then_inc(m["kT_done"], 1)
                    if a:
                        if isinstance(s, int) and s == 0:
                            turn_x(0, 0)
                        wait(pe, m["w_dma"], (s // NB + 1) * (16 * NWL))
                        wait(pe, m["xT_ready"], s + 1)
                        project(s, par, 0, 0, "q_done")
                    if b:
                        wait(pe, m["qT_ready"], n + 1)
                        wait(pe, m["kT_ready"], n + 1)
                        wait(pe, m["kprev_done"], n + 1)
                        wait(pe, m["o_ready"], n)
                        mk = at(mask, n % NB) if isinstance(n, int) else mask[:, bass.ds(n % NB, 1), :].rearrange("p a k -> p (a k)")
                        for hp in range(2):
                            pe.matmul(R[3][:, hp, :], identb[:], mk.unsqueeze(1).broadcast_to([P, PAIRS, 2 * WIN]),
                                      start=True, stop=False, skip_group_check=True)
                        for i in range(PAIRS):
                            for hp in range(2):
                                r = slice(LD * hp, LD * (hp + 1))
                                for w in range(NW):
                                    last = pe.matmul(R[3][WIN * w:WIN * (w + 1), hp, 2 * WIN * i:2 * WIN * (i + 1)],
                                                     qT[r, i, WIN * w:WIN * (w + 1)],
                                                     kT[r, 1 - par, i, WIN * w:WIN * (w + 2)],
                                                     start=False, stop=True, skip_group_check=True)
                        last.then_inc(m["s_done"], 1)
                    if c:
                        wait(pe, m["xn_done"], k + 1)
                        wait(pe, m["kT_ready"], min(k + 2, NT) if isinstance(k, int) else k + 2)
                        if isinstance(k, int) and k == NT - 1:
                            wait(pe, m["x2_done"], NT)
                        pe.transpose(flat[2][:, 0:P], xn[:], ident[:]).then_inc(m["xnT_done"], 1)
                    if a:
                        wait(pe, m["qT_ready"], s)
                        project(s, par, 1, 1, "k_done")
                        wait(pe, m["kT_ready"], s)
                        wait(pe, m["xnT_ready"], s - 1)
                        project(s, par, 2, 2, "v_done")
                    if c:
                        wait(pe, m["xnT_ready"], k + 1)
                        if a:
                            wait(pe, m["tq_done"], s + 1)
                        else:
                            wait(pe, m["x3_done"], k + NB)
                        for i in range(2):
                            w = at(w1, wp(k)) if isinstance(k, int) else w1[:, bass.ds(wp(k), 1), :].rearrange("p a f -> p (a f)")
                            last = pe.matmul(R[0][:, i, 0:FF], xnT[:], w[:, FF * i:FF * (i + 1)], start=True, stop=True)
                        last.then_inc(m["h_done"], 1)
                    if b:
                        wait(pe, m["exp_done"], n + 1)
                        if a:
                            wait(pe, m["tk_done"], s + 1)
                        for i in range(PAIRS):
                            last = pe.transpose(flat[1][:, P * i:P * (i + 1)], pr[:, i].rearrange("p a b -> p (a b)"), ident[:])
                        last.then_inc(m["pT_done"], 1)
                        wait(pe, m["pT_ready"], n + 1)
                        wait(pe, m["v2_dma"], (n + 1) * 160)
                        for i in range(PAIRS):
                            for w in range(NW):
                                last = pe.matmul(flat[3][WIN * w:WIN * (w + 1), P * i:P * (i + 1)],
                                                 prT[:, i, WIN * w:WIN * (w + 1)], v2[:, w, :, i, :], start=True, stop=True,
                                                 skip_group_check=True)
                        last.then_inc(m["pv2_done"], 1)
                    if c:
                        wait(pe, m["g_done"], k + 1)
                        if a:
                            wait(pe, m["v_ready"], s + 1)
                        for i, (o, w) in enumerate(FC):
                            last = pe.transpose(flat[2][0:w, P * i:P * (i + 1)], gs[:, o:o + w], ident[:])
                        last.then_inc(m["gT_done"], 1)
                    if b:
                        wait(pe, m["o_ready"], n + 1)
                        for i in range(PAIRS):
                            last = pe.transpose(flat[1][:, P * i:P * (i + 1)], ot[:, P * i:P * (i + 1)], ident[:])
                        last.then_inc(m["oT_done"], 1)
                    if c:
                        wait(pe, m["gT_ready"], k + 1)
                        w = w2[:, wp(k), :] if isinstance(k, int) else w2[:, bass.ds(wp(k), 1), :].rearrange("p a f -> p (a f)")
                        for i, (o, r) in enumerate(FC):
                            last = pe.matmul(flat[0][:, 0:D], gT[0:r, i, :], w[0:r, D * i:D * (i + 1)],
                                             start=(i == 0), stop=(i == 2))
                        last.then_inc(m["w2_done"], 1)
                    if b:
                        wait(pe, m["oT_ready"], n + 1)
                        wait(pe, m["gT_ready"], n)
                        w = wo[:, wp(n), :] if isinstance(n, int) else wo[:, bass.ds(wp(n), 1), :].rearrange("p a f -> p (a f)")
                        for i in range(PAIRS):
                            last = pe.matmul(flat[2][:, 0:D], otT[:, i, :], w[:, D * i:D * (i + 1)],
                                             start=(i == 0), stop=(i == PAIRS - 1))
                        last.then_inc(m["wo_done"], 1)
                    if a and not isinstance(s, int):
                        turn_x(s + 1, 1 - par)
                    elif a and s + 1 < NT:
                        turn_x(s + 1, 1 - par)

                steps(pe, step)

            @block.scalar
            def _(act):
                def copy(dst, src, ready):
                    act.activation(dst, src, ACT.Copy).then_inc(m[ready], 1)

                def xT_out(n, par):
                    wait(act, m["xT_done"], n + 1)
                    copy(xsT[:, par, :], flat[0][:, 0:P], "xT_ready")

                def step(s, par):
                    a, b, c = stages(s)
                    n, k = s - 1, s - 2
                    if isinstance(s, int) and s == 0:
                        xT_out(0, 0)
                    if b:
                        wait(act, m["qT_done"], n + 1)
                        wait(act, m["s_done"], n)
                        copy(qT[:].rearrange("p a b -> p (a b)"), flat[1], "qT_ready")
                        wait(act, m["kT_done"], n + 1)
                        wait(act, m["s_done"], n - 1)
                        wait(act, m["kprev_done"], n)
                        copy(kT[:, 1 - par, :, WIN:WIN + P], flat[2].rearrange("p (a b) -> p a b", b=P), "kT_ready")
                    if a:
                        wait(act, m["q_done"], s + 1)
                        wait(act, m["ssq_done"], 2 * s - 1)
                        act.activation(sq[:, 0, :], flat[0], ACT.Square).then_inc(m["sq_done"], 1)
                        wait(act, m["k_done"], s + 1)
                        wait(act, m["ssq_done"], 2 * s)
                        act.activation(sq[:, 1, :], flat[1], ACT.Square).then_inc(m["sq_done"], 1)
                    if b:
                        wait(act, m["sub_done"], n + 1)
                        p = pr[:].rearrange("p a b c -> p (a b c)")
                        act.activation(p, p, ACT.Exp, scale=QK_SCALE).then_inc(m["exp_done"], 1)
                    if a:
                        wait(act, m["v_done"], s + 1)
                        wait(act, m["v2_dma"], s * 160)
                        act.activation(vs[:, par, :].rearrange("p (hp i d) -> p hp i d", hp=2, d=LD),
                                       flat[2].rearrange("p (i hp d) -> p hp i d", hp=2, d=LD), ACT.Copy)\
                           .then_inc(m["v_ready"], 1)
                    if b:
                        wait(act, m["pT_done"], n + 1)
                        wait(act, m["pv2_done"], n)
                        copy(prT[:].rearrange("p a b -> p (a b)"), flat[1], "pT_ready")
                    if c:
                        wait(act, m["hb_done"], k + 1)
                        act.activation(hs[:, 1, :], hs[:, 1, :], ACT.Gelu).then_inc(m["gelu_done"], 1)
                        wait(act, m["gT_done"], k + 1)
                        wait(act, m["w2_done"], k)
                        act.activation(gT[:, 0:2, :], flat[2][:, 0:2 * P].rearrange("p (a b) -> p a b", b=P), ACT.Copy)
                        w = FC[2][1]
                        act.activation(gT[0:w, 2, :], flat[2][0:w, 2 * P:3 * P], ACT.Copy).then_inc(m["gT_ready"], 1)
                    if b:
                        wait(act, m["oT_done"], n + 1)
                        wait(act, m["wo_done"], n)
                        copy(otT[:].rearrange("p a b -> p (a b)"), flat[1], "oT_ready")
                    if a and (not isinstance(s, int) or s + 1 < NT):
                        xT_out(s + 1, 1 - par)

                steps(act, step)

            @block.gpsimd
            def _(pool):
                def table(n, par):
                    wait(pool, m["w_dma"], (n // NB + 1) * (16 * NWL))
                    wait(pool, m["tk_done"], n - 1)
                    if isinstance(n, int):
                        r, sc = rope[:, n % NB, :], scale_rows[:, wp(n), :]
                    else:
                        r = rope[:, bass.ds(n % NB, 1), :].rearrange("p a f -> p (a f)")
                        sc = scale_rows[:, bass.ds(wp(n), 1), :].rearrange("p a f -> p (a f)")
                    pool.tensor_tensor(tab[:, par].rearrange("p a b -> p (a b)"), r, sc, ALU.mult).then_inc(m["tab_done"], 1)

                def step(s, par):
                    a, b, c = stages(s)
                    n, k = s - 1, s - 2
                    if isinstance(s, int) and s == 0:
                        table(0, 0)
                    if b:
                        wait(pool, m["kT_ready"], n)
                        wait(pool, m["s_done"], n - 1)
                        f = has_prev[:, n % NB:n % NB + 1] if isinstance(n, int) else has_prev[:, bass.ds(n % NB, 1)]
                        pool.tensor_tensor(kT[:, 1 - par, :, 0:WIN], kT[:, par, :, P:P + WIN],
                                           f.unsqueeze(2).broadcast_to([P, PAIRS, WIN]), ALU.mult)\
                            .then_inc(m["kprev_done"], 1)
                    if c:
                        wait(pool, m["lnv_done"], k + 1)
                        take_waits(pool, m["pool_taken"])
                        pool.tensor_scalar(var[:], mv[:, 1:2], 1e-5, None, ALU.add).then_inc(m["eps_done"], 1)
                        wait(pool, m["eps_done"], k + 1)
                        pool.tensor_tensor(rstd[:], var[:], half1[:, 0:1], ALU.pow).then_inc(m["rstd_done"], 1)
                        wait(pool, m["x2_done"], k + 1)
                        wait(pool, m["x3_done"], k + NB)
                        if isinstance(k, int):
                            x, bb = xm[:, k % NB + 1, :], b2_rows[:, wp(k), :]
                        else:
                            x = xm[:, bass.ds(k % NB + 1, 1), :].rearrange("p a f -> p (a f)")
                            bb = b2_rows[:, bass.ds(wp(k), 1), :].rearrange("p a f -> p (a f)")
                        pool.tensor_tensor(xmb[:], x, bb, ALU.add).then_inc(m["xmb_done"], 1)
                    if a:
                        for i in range(2):
                            wait(pool, m["ssq_done"], 2 * s + 1 + i)
                            take_waits(pool, m["pool_taken"])
                            pool.tensor_scalar(ssq[:, i, :], ssq[:, i, :], 1e-24, None, ALU.max).then_inc(m["clamp_done"], 1)
                            wait(pool, m["clamp_done"], 2 * s + 1 + i)
                            pool.tensor_tensor(rnorm[:, i, :], ssq[:, i, :], half1[:, 0:LH], ALU.pow).then_inc(m["rn_done"], 1)
                            wait(pool, m["tq_done" if i == 0 else "tk_done"], s + 1)
                            pool.tensor_tensor(t1[:, i, :], t1[:, i, :], t2[:, i, :], ALU.add).then_inc(m["add_done"], 1)
                            wait(pool, m["add_done"], 2 * s + 1 + i)
                            wait(pool, m["rn_done"], 2 * s + 1 + i)
                            wait(pool, m["qT_done" if i == 0 else "kT_done"], s)
                            pool.tensor_tensor(qk[:, i, :].rearrange("p (h d) -> p h d", d=LD),
                                               t1[:, i, :].rearrange("p (h d) -> p h d", d=LD),
                                               rnorm[:, i, :].unsqueeze(2).broadcast_to([P, LH, LD]), ALU.mult)\
                                .then_inc(m["qk_done"], 1)
                    if a and (not isinstance(s, int) or s + 1 < NT):
                        table(s + 1, 1 - par)

                steps(pool, step)

            @block.vector
            def _(dve):
                def rotate(s, par, i, bank, done):
                    wait(dve, m["sq_done"], 2 * s + 1 + i)
                    wait(dve, m["tab_done"], s + 1)
                    wait(dve, m["qk_done"], 2 * s - 1 + i)
                    q = flat[bank].rearrange("p (h d) -> p h d", d=LD)
                    o1 = t1[:, i, :].rearrange("p (h d) -> p h d", d=LD)
                    o2 = t2[:, i, :].rearrange("p (h d) -> p h d", d=LD)
                    tb = lambda row, lo, hi: tab[:, par, row, lo:hi].unsqueeze(1).broadcast_to([P, LH, hi - lo])
                    dve.tensor_tensor(o1, q, tb(2 * i, 0, LD), ALU.mult)
                    hd = LD // 2
                    dve.tensor_tensor(o2[:, :, 0:hd], q[:, :, hd:LD], tb(2 * i + 1, 0, hd), ALU.mult)
                    dve.tensor_tensor(o2[:, :, hd:LD], q[:, :, 0:hd], tb(2 * i + 1, hd, LD), ALU.mult).then_inc(m[done], 1)
                    dve.tensor_reduce(ssq[:, i, :], sq[:, i, :].rearrange("p (h d) -> p h d", d=LD), AX.X, ALU.add)\
                       .then_inc(m["ssq_done"], 1)

                def step(s, par):
                    a, b, c = stages(s)
                    n, k = s - 1, s - 2
                    if c:
                        wait(dve, m["xs_f_dma"], (k + 1) * 48)
                        dve.bn_stats(bn[:], xs_f[:]).then_inc(m["st_done"], 1)
                        wait(dve, m["st_done"], k + 1)
                        wait(dve, m["rstd_done"], k)
                        take_waits(dve, m["dve_taken"])
                        dve.bn_aggr(mv[:], bn[:]).then_inc(m["lnv_done"], 1)
                    if a:
                        rotate(s, par, 0, 0, "tq_done")
                    if c:
                        wait(dve, m["rstd_done"], k + 1)
                        wait(dve, m["lnv_done"], k + 1)
                        wait(dve, m["xnT_done"], k)
                        dve.tensor_scalar(xn[:], xs_f[:], mv[:, 0:1], rstd[:, 0:1], ALU.subtract, ALU.mult)\
                           .then_inc(m["xn_done"], 1)
                    if b:
                        wait(dve, m["s_done"], n + 1)
                        dve.tensor_reduce(mx[:], R[3][:].rearrange("p a (i k) -> p a i k", k=2 * WIN), AX.X, ALU.max)\
                           .then_inc(m["mx_done"], 1)
                        wait(dve, m["mx_done"], n + 1)
                        wait(dve, m["pT_done"], n)
                        dve.tensor_tensor(pr[:].rearrange("p i a k -> p a i k"),
                                          R[3][:].rearrange("p a (i k) -> p a i k", k=2 * WIN),
                                          mx[:].unsqueeze(3).broadcast_to([P, 2, PAIRS, 2 * WIN]), ALU.subtract)\
                           .then_inc(m["sub_done"], 1)
                    if c:
                        wait(dve, m["xnT_done"], k + 1)
                        wait(dve, m["h_done"], k)
                        l = ln_cols[:, wp(k), :] if isinstance(k, int) else ln_cols[:, bass.ds(wp(k), 1), :].rearrange("p a f -> p (a f)")
                        dve.tensor_scalar(xnT[:], flat[2][:, 0:P], l[:, 0:1], l[:, 1:2], ALU.mult, ALU.add)\
                           .then_inc(m["xnT_ready"], 1)
                    if a:
                        rotate(s, par, 1, 1, "tk_done")
                    if c:
                        wait(dve, m["h_done"], k + 1)
                        wait(dve, m["g_done"], k)
                        bb = b1_rows[:, wp(k), :] if isinstance(k, int) else b1_rows[:, bass.ds(wp(k), 1), :].rearrange("p a f -> p (a f)")
                        dve.tensor_tensor(hs[:], R[0][:, :, 0:FF], bb.rearrange("p (a f) -> p a f", a=2), ALU.add)\
                           .then_inc(m["hb_done"], 1)
                    if b:
                        wait(dve, m["exp_done"], n + 1)
                        wait(dve, m["rden_done"], n)
                        dve.tensor_reduce(den[:], pr[:].rearrange("p i a k -> p (i a) k"), AX.X, ALU.add).then_inc(m["sum_done"], 1)
                        wait(dve, m["sum_done"], n + 1)
                        wait(dve, m["o_ready"], n)
                        dve.reciprocal(rden[:], den[:]).then_inc(m["rden_done"], 1)
                    if c:
                        wait(dve, m["gelu_done"], k + 1)
                        wait(dve, m["gT_done"], k)
                        dve.tensor_tensor(gs[:], hs[:, 0, :], hs[:, 1, :], ALU.mult).then_inc(m["g_done"], 1)
                    if b:
                        wait(dve, m["pv2_done"], n + 1)
                        wait(dve, m["rden_done"], n + 1)
                        wait(dve, m["oT_done"], n)
                        dve.tensor_tensor(ot[:].rearrange("p (h d) -> p h d", d=LD), flat[3].rearrange("p (h d) -> p h d", d=LD),
                                          rden[:].unsqueeze(2).broadcast_to([P, LH, LD]), ALU.mult).then_inc(m["o_ready"], 1)
                    if c:
                        wait(dve, m["w2_done"], k + 1)
                        wait(dve, m["xmb_done"], k + 1)
                        for q in range(2):
                            dve.wait_ge(xs_a_dma[q], ((k + 2 - q) // 2) * 48) if not isinstance(k, int) or k + 2 - q >= 2 else None
                        o = xa[:, k % NB + 1, :] if isinstance(k, int) else xa[:, bass.ds(k % NB + 1, 1), :].rearrange("p a f -> p (a f)")
                        dve.tensor_tensor(o, flat[0][:, 0:D], xmb[:], ALU.add).then_inc(m["x3_done"], 1)
                    if b:
                        wait(dve, m["wo_done"], n + 1)
                        if isinstance(n, int):
                            o, x = xm[:, n % NB + 1, :], xa[:, n % NB + 1, :]
                        else:
                            o = xm[:, bass.ds(n % NB + 1, 1), :].rearrange("p a f -> p (a f)")
                            x = xa[:, bass.ds(n % NB + 1, 1), :].rearrange("p a f -> p (a f)")
                        dve.tensor_tensor(o, flat[2][:, 0:D], x, ALU.add).then_inc(m["x2_done"], 1)

                steps(dve, step)

            @block.sync
            def _(sp):
                def load(l):
                    par = l % 2
                    def vec(name, lo, n):
                        return io[name][l:l + 1, lo:lo + n] if isinstance(l, int) else io[name][bass.ds(l, 1), lo:lo + n]
                    def mat(name, r0, r1):
                        a = io[name]
                        return a[l, r0:r1, :] if isinstance(l, int) else a[bass.ds(l, 1), r0:r1, :].rearrange("a r c -> (a r) c")
                    def to(tile, lo, hi, rows=P):
                        if isinstance(l, int):
                            return tile[0:rows, par, lo:hi]
                        return tile[0:rows, bass.ds(par, 1), lo:hi].rearrange("p a f -> p (a f)")
                    wide = lambda v: v.rearrange("a f -> (a f)").partition_broadcast(P)
                    hd = LD // 2
                    jobs = (
                        (to(wqkv, 0, 3 * INNER), mat("Wqkv", 0, D)),
                        (to(wo, 0, PAIRS * D).rearrange("p (c n) -> p c n", n=D),
                         mat("Wo2", 0, INNER).rearrange("(c p) n -> p c n", p=P)),
                        (to(w1, 0, 2 * FF), mat("W1", 0, D)),
                        (to(w2, 0, 2 * D).rearrange("p (c n) -> p c n", n=D),
                         mat("W2", 0, 2 * P).rearrange("(c p) n -> p c n", p=P)),
                        (to(w2, 2 * D, 3 * D, FF - 2 * P), mat("W2", 2 * P, FF)),
                        (to(b1_rows, 0, 2 * FF), wide(vec("b1", 0, 2 * FF))),
                        (to(b2_rows, 0, D), wide(vec("b2", 0, D))),
                        (to(ln_cols, 0, 1), vec("ln_g", 0, D).rearrange("a f -> f a")),
                        (to(ln_cols, 1, 2), vec("ln_b", 0, D).rearrange("a f -> f a")),
                    ) + tuple(
                        (to(scale_rows, 2 * LD * i + o, 2 * LD * i + o + w), wide(vec(name, lo, w)))
                        for i, name in enumerate(("q_scale", "k_scale"))
                        for o, lo, w in ((0, 0, LD), (LD, hd, hd), (LD + hd, 0, hd))
                    )
                    for dst, src in jobs:
                        sp.dma_start(dst, src).then_inc(m["w_dma"], 16)
                    return len(jobs)

                def shift(dst, src, n, done):
                    b = n % NB
                    take_waits(sp, m["sp_taken"])
                    if isinstance(n, int):
                        own, before = src[:, b + 1, :], src[P - 1:P, b, D // 2:D]
                    else:
                        own = src[:, bass.ds(b + 1, 1), :].rearrange("p a f -> p (a f)")
                        before = src[P - 1:P, bass.ds(b, 1), D // 2:D].rearrange("p a f -> p (a f)")
                    sp.dma_start(dst[:, 0:D // 2], own[:, 0:D // 2]).then_inc(done, 16)
                    sp.dma_start(dst[1:P, D // 2:D], own[0:P - 1, D // 2:D]).then_inc(done, 16)
                    sp.dma_start(dst[0:1, D // 2:D], before).then_inc(done, 16)

                def shift_a(n, par):
                    wait(sp, m["x3_done"], n + 1)
                    wait(sp, m["xT_done"], n - 1)
                    shift(xs_a[:, par, :], xa, n, xs_a_dma[par])

                def step(s, par):
                    a, b, c = stages(s)
                    n, k = s - 1, s - 2
                    if a and (not isinstance(s, int) or s + 1 < NT):
                        shift_a(s + 1, 1 - par)
                    if a:
                        wait(sp, m["v_ready"], s + 1)
                        wait(sp, m["pv2_done"], s)
                        for hp in range(2):
                            cols = slice(PAIRS * LD * hp, PAIRS * LD * (hp + 1))
                            r = 2 * WIN * hp
                            v = lambda lo, hi, w: v2[r + lo:r + hi, w, hp, :, :].rearrange("p i d -> p (i d)")
                            sp.dma_start(v(0, WIN, 0), vs[P - WIN:P, 1 - par, cols]).then_inc(m["v2_dma"], 16)
                            sp.dma_start(v(WIN, 2 * WIN, 0), vs[0:WIN, par, cols]).then_inc(m["v2_dma"], 16)
                            for w in range(1, NW):
                                sp.dma_start(v(0, 2 * WIN, w), vs[WIN * (w - 1):WIN * (w + 1), par, cols])\
                                  .then_inc(m["v2_dma"], 16)
                    if b:
                        wait(sp, m["x2_done"], n + 1)
                        take_waits(sp, m["sp_taken"])
                        wait(sp, m["xn_done"], n)
                        shift(xs_f, xm, n, m["xs_f_dma"])

                def pair(i):
                    step(i * 2, 0)
                    step(i * 2 + 1, 1)

                half = NB // 2
                assert load(0) == NWL
                shift_a(0, 0)
                for s in range(4):
                    step(s, s % 2)
                    if s == 1:
                        load(1)
                with sp.Fori(2, half) as i:
                    pair(i)
                with sp.Fori(1, LAYERS - 1) as l:
                    pair(l * half)
                    sp.wait_ge(m["x3_done"], NB * l + NB)
                    take_waits(sp, m["sp_taken"])
                    load(l + 1)
                    with sp.Fori(1, half) as i:
                        pair(l * half + i)
                with sp.Fori((LAYERS - 1) * half, LAYERS * half - 1) as i:
                    pair(i)
                for s in range(NT - 2, NT + 2):
                    step(s, s % 2)

        with nc.Block() as block:
            @block.sync
            def _(sp):
                sp.dma_start(xm[:, 1:NB + 1, :], io["x1"].rearrange("(b p) d -> p b d", p=P)).then_inc(m["init_dma"], 16)
                sp.wait_ge(m["init_dve"], 4)
                sp.dma_start(io["out"].rearrange("a (b p) d -> p (a b) d", p=P), xa[:, 1:NB + 1, :]).then_inc(m["out_dma"], 16)
                sp.wait_ge(m["out_dma"], 16)

            @block.vector
            def _(dve):
                dve.wait_ge(m["init_dma"], 16 * 5)
                dve.tensor_tensor(xa[:, 1:NB + 1, :], xa[:, 1:NB + 1, :], xm[:, 1:NB + 1, :], ALU.add)\
                   .then_inc(m["init_dve"], 1)


def global_constants():
    r = np.arange(P)
    term = r % 64 // G
    return {
        "ident": np.eye(P, dtype=np.float32),
        "tmask": np.stack([(term == 0) | (term == 3), term == 1, term == 2], 1).astype(np.float32),
        "dmask": (r[:, None] % G == np.arange(G)[None]).astype(np.float32),
    }


def local_constants():
    f = np.float32
    half = np.arange(0, LD, 2, dtype=f)
    freqs = np.arange(S, dtype=f)[:, None] * (f(1.0) / f(10000.0) ** (half / f(LD)))[None, :]
    freqs = np.concatenate([freqs, freqs], -1)
    base = (half + f(0.4 * LD)) / f(1.4 * LD)
    power = (np.arange(S, dtype=f) - f(S // 2)) / f(WIN // 2)
    scale = base[None, :] ** power[:, None]
    scale = np.concatenate([scale, scale], -1)
    cos, sin = np.cos(freqs), np.sin(freqs)
    sign = np.where(np.arange(LD) < LD // 2, f(-1), f(1))[None, :]
    inv = f(1.0) / scale
    rope = np.stack([cos * scale, sin * scale * sign, cos * inv, sin * inv * sign], 1).astype(f)
    rope = rope.reshape(NB, P, 4 * LD).transpose(1, 0, 2)
    q = np.arange(P) % WIN
    key = np.arange(2 * WIN) - WIN
    banned = (q[:, None] < key[None]) | (q[:, None] > key[None] + WIN)
    first = banned | ((np.arange(P) < WIN)[:, None] & (key < 0)[None])
    return {"rope": np.ascontiguousarray(rope),
            "mask": np.stack([np.where(b, f(-1e30), f(0)) for b in (first, banned)], 1).astype(f)}


def program(nc, x, wq, bq, wk, bk, wv, bv, wo, bo, rel_w, rel_b, logical_bias, gate_w, gate_b,
            wqkv, q_scale, k_scale, wo2, ln_g, ln_b, w1, b1, w2, b2, ident, tmask, dmask, rope, mask, out):
    io = {
        "x": x, "Wq": wq, "bq": bq, "Wk": wk, "bk": bk, "Wv": wv, "bv": bv, "Wo": wo, "bo": bo, "rel_W": rel_w,
        "rel_b": rel_b, "logical_bias": logical_bias, "gate_W": gate_w, "gate_b": gate_b, "Wqkv": wqkv,
        "q_scale": q_scale, "k_scale": k_scale, "Wo2": wo2, "ln_g": ln_g, "ln_b": ln_b, "W1": w1, "b1": b1,
        "W2": w2, "b2": b2, "ident": ident, "tmask": tmask, "dmask": dmask, "rope": rope, "mask": mask, "out": out,
        "q_parts": nc.dram_tensor("q_parts", [3, D, S], BF16, kind="Internal").ap(),
        "k_parts": nc.dram_tensor("k_parts", [3, D, S], BF16, kind="Internal").ap(),
        "p_parts": nc.dram_tensor("p_parts", [NC_, 2, P, S], FP16, kind="Internal").ap(),
        "x1": nc.dram_tensor("x1", [S, D], F32, kind="Internal").ap(),
    }
    with ExitStack() as ctx:
        global_attention(nc, ctx, io)
    local_layers(nc, io)


_INS = [f"L0_attn_{n}" for n in ("hidden_states", "Wq", "bq", "Wk", "bk", "Wv", "bv", "Wo", "bo", "rel_W", "rel_b",
                                 "logical_bias", "gate_W", "gate_b")]
_INS += [f"L0_ffn_{n}" for n in ("Wqkv", "q_scale", "k_scale", "Wo", "ln_g", "ln_b", "W1", "b1", "W2", "b2")]


def kernel(**inputs):
    import numpy as _np
    import concourse.bacc as _bacc
    from concourse import mybir as _mybir
    from concourse.bass_utils import run_bass_kernel_spmd as _run

    nc = _bacc.Bacc("TRN2", target_bir_lowering=False, num_devices=1)
    given = {name: _np.ascontiguousarray(inputs[name]) for name in _INS}
    given.update(global_constants())
    given.update(local_constants())
    arrays, args = {}, []
    for name, a in given.items():
        arrays[f"in_{name}"] = a
        args.append(nc.dram_tensor(f"in_{name}", a.shape, _mybir.dt.from_np(a.dtype), kind="ExternalInput").ap())
    out = nc.dram_tensor("out_x", [1, S, D], F32, kind="ExternalOutput").ap()
    program(nc, *args, out)
    return _run(nc, [arrays], core_ids=[0]).results[0]["out_x"]
```

```python
from contextlib import ExitStack

import numpy as np
import concourse.bass as bass
from concourse import mybir

ALU = mybir.AluOpType
ACT = mybir.ActivationFunctionType
F32 = mybir.dt.float32
BF16 = mybir.dt.bfloat16
FP16 = mybir.dt.float16
AX = mybir.AxisListType

P = 128
S = 2048
D = 128
NB = S // P
H, HD = 16, 8
HH = H // 2
G = 16
NG = P // G
CH = 64
NC_ = S // CH
TERMS = ((0, 0), (0, 1), (0, 2), (1, 0), (1, 1), (2, 0))
GUARD_ROW = len(TERMS) * HD
LEAD = 22


LAYERS = 6
NT = LAYERS * NB
LH, LD = 16, 64
PAIRS = LH // 2
INNER = LH * LD
WIN = 32
NW = P // WIN
FF = D * 4 * 2 // 3
QK_SCALE = 8.0
FC = ((0, P), (P, P), (2 * P, FF - 2 * P))
NWL = 17


def take_waits(eng, count):
    eng.sem_inc(count, 1)


def prepare(nc, io, keep):
    with ExitStack() as ctx:
        sb = lambda n, s, d=F32: ctx.enter_context(nc.sbuf_tensor(n, s, d))
        sem = lambda n: ctx.enter_context(nc.semaphore(n))
        x_in, q_parts = keep["x_res"], keep["q_parts"]
        ident, tmask, dmask = keep["ident"], keep["tmask"], keep["dmask"]
        bn = sb("bn", [P, NB, 6])
        mv = sb("mv", [P, NB, 2])
        rstd = sb("rstd", [P, NB])
        half = sb("half", [P, NB])
        xn = sb("xn", [P, NB, D])
        xnT = sb("xnT", [P, S])
        w_nat = sb("w_nat", [P, 4, D])
        wT = sb("wT", [P, 4, D])
        gate_nat = sb("gate_nat", [H, D])
        rel_nat = sb("rel_nat", [3, 2, D])
        smallT = sb("smallT", [P, H + 6])
        bq = sb("bq", [P, 1])
        bk = sb("bk", [P, 1])
        bv_rows = sb("bv_rows", [P, D])
        bo_rows = sb("bo_rows", [P, D])
        gate_b_rows = sb("gate_b_rows", [P, H])
        rel_b_rows = sb("rel_b_rows", [P, 3])
        lb_rows = sb("lb_rows", [P, H, 3])
        w_lj = sb("w_lj", [P, 2, P])
        b_drel = sb("b_drel", [P, 2])
        li_raw = sb("li_raw", [P, NC_, 4])
        d_lb = sb("d_lb", [P, H])
        full = sb("full", [P, S])
        rest = sb("rest", [P, S])
        part = sb("part", [P, 3, S], BF16)
        tok = sb("tok", [P, NB, H + 4])
        pick8 = sb("pick8", [P, NG, P // G, G])
        pick2 = sb("pick2", [P, 2, 2, G, CH // G])
        w_tok = sb("w_tok", [P, H + 4])
        ps = ctx.enter_context(nc.psum_tensor("ps_prep", [P, 8, 512], F32))

        loads = sem("prep_loads")
        mm = sem("prep_mm")
        ev = sem("prep_ev")
        v = sem("prep_v")
        act = sem("prep_act")
        rs = sem("prep_rstd")
        picks = sem("prep_picks")
        pool = sem("prep_pool")
        stored = sem("prep_stored")
        XN_READY, DIFF_READY, Q_SPLIT, K_SPLIT, GATE_X = "xn", "diff", "q", "k", "g"
        marks = {}

        block = ctx.enter_context(nc.Block())

        @block.vector
        def _(dve):
            n = [0]

            def link(ins):
                n[0] += 1
                ins.then_inc(v, 1)
                dve.wait_ge(v, n[0])

            dve.wait_ge(loads, 16 * LOADS)
            for b in range(NB):
                last = dve.bn_stats(bn[:, b, :], x_in[:, b, :])
            link(last)
            for b in range(NB):
                last = dve.bn_aggr(mv[:, b, :], bn[:, b, :])
            link(last)
            marks["var"] = n[0]
            dve.wait_ge(rs, 1)
            link(dve.tensor_tensor(xn[:], x_in[:], mv[:, :, 0:1].broadcast_to([P, NB, D]), ALU.subtract))
            link(dve.tensor_tensor(xn[:], xn[:], rstd[:].unsqueeze(2).broadcast_to([P, NB, D]), ALU.mult))
            marks[XN_READY] = n[0]
            link(dve.tensor_tensor(x_in[:], x_in[:], bo_rows[:].unsqueeze(1).broadcast_to([P, NB, D]), ALU.add))

            group = [0]

            def bank():
                group[0] += 1
                dve.wait_ge(mm, group[0])
                return ps[:, (group[0] - 1) % 8, :]

            dve.tensor_copy(wT[:].rearrange("p a b -> p (a b)"), bank()).then_inc(ev, 1)
            dve.tensor_copy(smallT[:], bank()[:, 0:H + 6]).then_inc(ev, 1)
            for c in range(4):
                dve.tensor_copy(xnT[:, 512 * c:512 * (c + 1)], bank()).then_inc(ev, 1)
            dve.wait_ge(ev, group[0])
            for half in range(2):
                o = H + 3 * half
                for c, (a, b) in enumerate(((1, 0), (0, 1), (2, 0), (2, 1))):
                    wa, wb = smallT[:, o + a:o + a + 1], smallT[:, o + b:o + b + 1]
                    if half == 0:
                        last = dve.tensor_tensor(w_tok[:, H + c:H + c + 1], wa, wb, ALU.subtract)
                    else:
                        k = c % 2
                        last = dve.tensor_tensor(w_lj[:, c // 2, CH * k:CH * (k + 1)], wa.broadcast_to([P, CH]),
                                                 wb.broadcast_to([P, CH]), ALU.subtract)
            link(last)
            link(dve.tensor_copy(w_tok[:, 0:H], smallT[:, 0:H]))
            marks[DIFF_READY] = n[0]
            for k in range(2):
                r = slice(CH * k, CH * (k + 1))
                dve.tensor_tensor(b_drel[r, 0:1], rel_b_rows[r, 1 - k:2 - k], rel_b_rows[r, k:k + 1], ALU.subtract)
                dve.tensor_tensor(b_drel[r, 1:2], rel_b_rows[r, 2:3], rel_b_rows[r, k:k + 1], ALU.subtract)
                last = dve.tensor_tensor(d_lb[r, :], lb_rows[r, :, k], lb_rows[r, :, 2], ALU.subtract)
            link(last)

            for name, bias, scale in ((Q_SPLIT, bq, HD ** -0.5), (K_SPLIT, bk, 1.0)):
                for c in range(4):
                    dve.tensor_scalar(full[:, 512 * c:512 * (c + 1)], bank(), bias[:, 0:1], scale,
                                      ALU.add, ALU.mult).then_inc(ev, 1)
                dve.wait_ge(ev, group[0])
                if name == K_SPLIT:
                    dve.wait_ge(stored, 16 * 3)
                link(dve.tensor_copy(part[:, 0, :], full[:]))
                link(dve.tensor_tensor(rest[:], full[:], part[:, 0, :], ALU.subtract))
                link(dve.tensor_copy(part[:, 1, :], rest[:]))
                link(dve.tensor_tensor(part[:, 2, :], rest[:], part[:, 1, :], ALU.subtract))
                marks[name] = n[0]
            for c in range(4):
                dve.tensor_tensor(keep["v9"][:, 4 * c:4 * (c + 1), :, 0:HD],
                                  bank().rearrange("p (b h d) -> p b h d", b=4, h=H),
                                  bv_rows[:].rearrange("p (h d) -> p h d", h=H).unsqueeze(1).broadcast_to([P, 4, H, HD]),
                                  ALU.add).then_inc(ev, 1)
            dve.memset(keep["v9"][:, :, :, HD:HD + 1], 1.0)
            for m in range(2):
                for c in range(4):
                    dve.tensor_copy(keep["lj"][:, m, 512 * c:512 * (c + 1)], bank()).then_inc(ev, 1)
            t3 = tok[:]
            dve.tensor_tensor(t3[:, :, 0:H], bank()[:, 0:NB * (H + 4)].rearrange("p (b h) -> p b h", h=H + 4)[:, :, 0:H],
                              gate_b_rows[:].unsqueeze(1).broadcast_to([P, NB, H]), ALU.add)
            dve.tensor_copy(t3[:, :, H:H + 4], ps[:, (group[0] - 1) % 8, 0:NB * (H + 4)]
                            .rearrange("p (b h) -> p b h", h=H + 4)[:, :, H:H + 4]).then_inc(ev, 1)
            dve.wait_ge(act, 1)
            link(dve.tensor_scalar(t3[:, :, 0:H], t3[:, :, 0:H], 1.0, None, ALU.add))
            link(dve.reciprocal(t3[:, :, 0:H], t3[:, :, 0:H]))
            marks["tok"] = n[0]
            dve.tensor_copy(li_raw[:].rearrange("p (b hf) f -> p hf b f", hf=2),
                            bank()[:, 0:4 * NC_].rearrange("p (hf b f) -> p hf b f", hf=2, f=4)).then_inc(ev, 1)
            dve.wait_ge(ev, group[0])
            for k in range(2):
                r = slice(CH * k, CH * (k + 1))
                for m in range(2):
                    dve.tensor_scalar(keep["li"][r, m, :], li_raw[r, :, 2 * m + k], b_drel[r, m:m + 1], None, ALU.add)
            full4 = full[:].rearrange("p (b g h) -> p g b h", g=NG, h=H)
            for c in range(4):
                last = dve.tensor_tensor(full4[:, 2 * c:2 * c + 2], bank().rearrange("p (g b h) -> p g b h", g=2, h=H),
                                         d_lb[:].unsqueeze(1).unsqueeze(1).broadcast_to([P, 2, NB, H]), ALU.mult)
                last.then_inc(ev, 1)
            dve.wait_ge(ev, group[0])
            dve.wait_ge(stored, 16 * 6)
            link(dve.tensor_copy(part[:, 0, :], full[:]))
            link(dve.tensor_tensor(rest[:], full[:], part[:, 0, :], ALU.subtract))
            link(dve.tensor_copy(part[:, 1, :], rest[:]))
            link(dve.tensor_tensor(part[:, 2, :], rest[:], part[:, 1, :], ALU.subtract))
            cc = keep["coef"][:].rearrange("p g h -> p (g h)")
            link(dve.tensor_scalar(cc, part[:, 0, :], tmask[:, 0:1], None, ALU.mult))
            link(dve.scalar_tensor_tensor(cc, part[:, 1, :], tmask[:, 1:2], cc, ALU.mult, ALU.add))
            link(dve.scalar_tensor_tensor(cc, part[:, 2, :], tmask[:, 2:3], cc, ALU.mult, ALU.add))
            link(dve.tensor_copy(keep["woT"][:], wT[:, 3, :]))

        @block.scalar
        def _(sc):
            sc.wait_ge(loads, 16 * LOADS)
            for k in range(2):
                last = sc.activation(pick2[:, :, k].rearrange("p hf i g -> p hf g i"),
                                     ident[:].rearrange("p (hf g i) -> p hf g i", hf=2, i=G), ACT.Copy)
            sc.activation(pick8[:], ident[:].rearrange("p (g i) -> p g i", i=G).unsqueeze(2)
                          .broadcast_to([P, NG, P // G, G]), ACT.Copy).then_inc(picks, 1)
            sc.wait_ge(ev, TOK_GROUP)
            sc.activation(tok[:, :, 0:H], tok[:, :, 0:H], ACT.Exp, scale=-1.0).then_inc(act, 1)

        @block.tensor
        def _(pe):
            n = [0]

            def bank():
                if n[0] >= 8:
                    pe.wait_ge(ev, n[0] - 7)
                n[0] += 1
                return ps[:, (n[0] - 1) % 8, :]

            pe.wait_ge(loads, 16 * LOADS)
            o = bank()
            for w in range(4):
                last = pe.transpose(o[:, D * w:D * (w + 1)], w_nat[:, w, :], ident[:])
            last.then_inc(mm, 1)
            o = bank()
            pe.transpose(o[:, 0:H], gate_nat[:], ident[0:H, 0:H])
            pe.transpose(o[:, H:H + 3], rel_nat[:, 0, :], ident[0:3, 0:3])
            pe.transpose(o[:, H + 3:H + 6], rel_nat[:, 1, :], ident[0:3, 0:3]).then_inc(mm, 1)
            pe.wait_ge(v, marks[XN_READY])
            for c in range(4):
                o = bank()
                for b in range(4):
                    last = pe.transpose(o[:, P * b:P * (b + 1)], xn[:, 4 * c + b, :], ident[:])
                last.then_inc(mm, 1)
            pe.wait_ge(ev, 6)
            for w in range(2):
                for c in range(4):
                    pe.matmul(bank(), wT[:, w, :], xnT[:, 512 * c:512 * (c + 1)], start=True, stop=True).then_inc(mm, 1)
            for c in range(4):
                o = bank()
                for b in range(4):
                    t = P * (4 * c + b)
                    last = pe.matmul(o[:, D * b:D * (b + 1)], xnT[:, t:t + P], wT[:, 2, :], start=True, stop=True)
                last.then_inc(mm, 1)
            pe.wait_ge(v, marks[DIFF_READY])
            for m in range(2):
                for c in range(4):
                    pe.matmul(bank(), w_lj[:, m, :], xnT[:, 512 * c:512 * (c + 1)], start=True, stop=True).then_inc(mm, 1)
            o = bank()
            assert n[0] == TOK_GROUP
            for b in range(NB):
                last = pe.matmul(o[:, (H + 4) * b:(H + 4) * (b + 1)], xnT[:, P * b:P * (b + 1)], w_tok[:], start=True, stop=True)
            last.then_inc(mm, 1)
            pe.wait_ge(picks, 1)
            pe.wait_ge(v, marks["tok"])
            o = bank()
            for hf in range(2):
                last = pe.matmul(o[:, 4 * NB * hf:4 * NB * (hf + 1)], pick2[:, hf].rearrange("p k i g -> p (k i g)"),
                                 tok[:, :, H:H + 4], start=True, stop=True)
            last.then_inc(mm, 1)
            for c in range(4):
                o = bank()
                for g in range(2):
                    last = pe.matmul(o[:, NB * H * g:NB * H * (g + 1)], pick8[:, 2 * c + g].rearrange("p k i -> p (k i)"),
                                     tok[:, :, 0:H], start=True, stop=True)
                last.then_inc(mm, 1)

        @block.gpsimd
        def _(g):
            g.wait_ge(v, marks["var"])
            g.tensor_scalar(mv[:, :, 1], mv[:, :, 1], 1e-5, None, ALU.add).then_inc(pool, 1)
            g.memset(half[:], -0.5).then_inc(pool, 1)
            g.wait_ge(pool, 2)
            g.tensor_tensor(rstd[:], mv[:, :, 1], half[:], ALU.pow).then_inc(rs, 1)
            n = 2
            g.wait_ge(rs, 1)
            for tile, value in ((keep["kst"][32:64, :, :], 1.0), (keep["kst"][96:128, :, :], 1.0),
                                (keep["zrow"][:], 0.0), (keep["qst"][:], 0.0)):
                g.memset(tile, value).then_inc(pool, 1)
                n += 1
                g.wait_ge(pool, n)

        @block.sync
        def _(sp):
            count = 0
            rows = lambda ap: ap.partition_broadcast(P)
            for dst, src in (
                (x_in[:], io["x"].rearrange("a (b p) d -> p (a b) d", p=P)), (ident[:], io["ident"]),
                (tmask[:], io["tmask"]), (dmask[:], io["dmask"]),
                (w_nat[:, 0, :], io["Wq"]), (w_nat[:, 1, :], io["Wk"]), (w_nat[:, 2, :], io["Wv"]),
                (w_nat[:, 3, :], io["Wo"]), (gate_nat[:], io["gate_W"]),
                (rel_nat[:], io["rel_W"].rearrange("k (a d) -> k a d", a=2)),
                (bq[:], io["bq"].unsqueeze(1)), (bk[:], io["bk"].unsqueeze(1)),
                (bv_rows[:], rows(io["bv"])), (bo_rows[:], rows(io["bo"])),
                (gate_b_rows[:], rows(io["gate_b"])), (rel_b_rows[:], rows(io["rel_b"])),
                (lb_rows[:], rows(io["logical_bias"])),
            ):
                sp.dma_start(dst, src).then_inc(loads, 16)
                count += 1
            assert count == LOADS
            sp.wait_ge(v, marks[Q_SPLIT])
            for a in range(3):
                sp.dma_start(q_parts[a], part[:, a, :]).then_inc(stored, 16)
            sp.wait_ge(v, marks[K_SPLIT])
            for a in range(3):
                sp.dma_start(io["k_parts"][a], part[:, a, :]).then_inc(stored, 16)
            sp.wait_ge(stored, 16 * 6)
            sp.wait_ge(pool, 5)
            for hp in range(2):
                for t, (_, b) in enumerate(TERMS):
                    r = 64 * hp + HD * t
                    src = io["k_parts"][b].rearrange("(pair hp d) s -> hp d pair s", hp=2, d=HD)[hp]
                    sp.dma_start(keep["kst"][r:r + HD, :, :], src).then_inc(stored, 16)
            for hp in range(2):
                for t, (a, _) in enumerate(TERMS):
                    src = q_parts[a].rearrange("(pair hp d) s -> hp d pair s", hp=2, d=HD)[hp]
                    sp.dma_start(io["q_stack"][hp, HD * t:HD * (t + 1)], src).then_inc(stored, 16)
                sp.dma_start(io["q_stack"][hp, GUARD_ROW:GUARD_ROW + 3].rearrange("r pair (b i) -> r (pair b) i", i=P),
                             keep["zrow"][:].unsqueeze(1).broadcast_to([3, H // 2 * NB, P])).then_inc(stored, 16)
            sp.wait_ge(stored, 16 * (18 + 14))


LOADS = 17
TOK_GROUP = 2 + 4 + 8 + 4 + 8 + 1


def attention(nc, io, keep):
    with ExitStack() as ctx:
        sb = lambda n, s, d=F32: ctx.enter_context(nc.sbuf_tensor(n, s, d))
        sem = lambda n: ctx.enter_context(nc.semaphore(n))
        kst, qst, v9, coef = keep["kst"], keep["qst"], keep["v9"], keep["coef"]
        lj, li, x_res, woT, ident, dmask = keep["lj"], keep["li"], keep["x_res"], keep["woT"], keep["ident"], keep["dmask"]
        zrow = keep["zrow"]
        pst = sb("pst", [P, 2, NG, S], FP16)
        diag = sb("diag", [P, 2, NG, H, G], BF16)
        prob = sb("prob", [P, 2, HH * P])
        colmax = sb("colmax", [P, 2, HH * P])
        rel_exp = sb("rel_exp", [P, 2, 2, 512])
        own = sb("own", [P, 2, 2, 1])
        rel_sum = sb("rel_sum", [P, 2, 512])
        rel_p = sb("rel_p", [P, 2, 512])
        stage = sb("stage", [P, 2, 2, S], FP16)
        rmax = sb("rmax", [P, HH])
        grest = sb("grest", [P, 2, HH])
        gpart = sb("gpart", [P, 3, HH], BF16)
        guard = sb("guard", [P, 2, 3, HH // 2])
        guardT = sb("guardT", [2 * 3 * HH // 2, P], BF16)
        outT = sb("outT", [P, 2, P])
        rden = sb("rden", [P, HH])
        heads = sb("heads", [P, D])
        headsT = sb("headsT", [P, D])
        x1 = sb("x1_sb", [P, D])
        psA = ctx.enter_context(nc.psum_tensor("psA", [P, 2, 512], F32))
        psB = ctx.enter_context(nc.psum_tensor("psB", [P, 2, 2, 512], F32))
        psO = ctx.enter_context(nc.psum_tensor("psO", [P, 512], F32))
        psM = ctx.enter_context(nc.psum_tensor("psM", [P, 512], F32))

        a_done = sem("a_done")
        a_read = sem("a_read")
        b_done = sem("b_done")
        e_done = sem("e_done")
        pv_done = sem("pv_done")
        o_read = sem("o_read")
        m_done = sem("m_done")
        m_read = sem("m_read")
        dch = sem("att_dve_chain")
        guard_in = sem("guard_in")
        guard_dma = sem("guard_dma")
        x1_dma = sem("x1_dma")
        re_done = sem("re_done")
        rc_first = sem("rc_first")
        rc_done = sem("rc_done")
        rs_done = sem("rs_done")
        rr_done = sem("rr_done")
        own_done = sem("own_done")
        r1_done = sem("r1_done")
        rp_done = sem("rp_done")
        rq_done = sem("rq_done")
        pst_dma = [sem(f"pst_dma{i}") for i in range(4)]
        p_dma = [sem(f"p_dma{i}") for i in range(2)]
        p_parts = io["p_parts"]
        q_dma = [sem(f"q_dma{i}") for i in range(2)]
        diag_done = sem("diag_done")
        zero_o = sem("zero_o")
        pool_waits = sem("pool_waits")
        sp_waits = sem("sp_waits")
        QD = 2
        PD = 2 * 2

        def unit_events(ul, first, last):
            ev = {}
            if not (first and ul == 0):
                ev[2] = "out"
                if ul % 2 == 0:
                    ev[4], ev[6] = "heads", "proj"
            if not (last and ul == 3):
                ev[10], ev[11], ev[13] = "max0", "max1", "guard"
            return ev

        def events_before(it, ul, step, first, last):
            n = 3 if first else 20 * it
            for w in range(ul + 1):
                e = unit_events(w, first, last)
                n = n + sum(1 for k in e if w < ul or k < step)
            return n

        def differences(eng, q, par):
            for m in range(2):
                last = eng.tensor_scalar(rel_exp[:, q % 2, m, :], lj[:, m, 512 * q:512 * (q + 1)], own[:, par, m, :],
                                         80.0, ALU.add, ALU.min)
            return last

        block = ctx.enter_context(nc.Block())

        @block.tensor
        def _(pe):
            def scores(dst, par, half, jb):
                for hl in range(HH):
                    h = HH * half + hl
                    pe.matmul(dst[:, hl // 4, P * (hl % 4):P * (hl % 4 + 1)], kst[:, h // 2, P * jb:P * (jb + 1)],
                              qst[:, par, h, :], start=(hl % 4 == 0), stop=False, skip_group_check=True)
                for g in range(NG):
                    for q in range(2):
                        o = dst[:, q, :].rearrange("p (h i) -> p h i", h=4)[:, :, G * g:G * (g + 1)]
                        h0 = HH * half + 4 * q
                        last = pe.matmul(o, pst[:, par, g, P * jb:P * (jb + 1)], diag[:, par, g, h0:h0 + 4, :],
                                         start=False, stop=(g == NG - 1), skip_group_check=True)
                return last

            def a_tile(a, ul, jb, block_no):
                pe.wait_ge(a_read, a) if not (isinstance(a, int) and a == 0) else None
                if ul % 2 == 0 and jb == 0:
                    par = (ul // 2) % 2
                    for c in range(2):
                        pe.wait_ge(pst_dma[2 * par + c], block_times(block_no) * 16 * PD)
                    pe.wait_ge(q_dma[par], block_times(block_no) * 16 * QD)
                    pe.wait_ge(diag_done, block_no + 1)
                scores(psA, (ul // 2) % 2, ul % 2, jb).then_inc(a_done, 1)

            def block_times(n):
                return n // 2 + 1

            def values(b, jb, half, first_unit_wait):
                pe.wait_ge(e_done, b + 1)
                if jb == 0 and not (isinstance(first_unit_wait, int) and first_unit_wait == 0):
                    pe.wait_ge(o_read, first_unit_wait)
                for hl in range(HH):
                    s, c = hl // 4, hl % 4
                    last = pe.matmul(psO[32 * c:32 * c + HD + 1, P * s:P * (s + 1)], v9[:, jb, HH * half + hl, :],
                                     prob[:, jb % 2, P * hl:P * (hl + 1)], start=(jb == 0 and s == 0),
                                     stop=(jb == NB - 1), skip_group_check=True)
                last.then_inc(pv_done, 1)

            def through_m(kind, n, unit, ul):
                pe.wait_ge(m_read, n) if not (isinstance(n, int) and n == 0) else None
                if kind in ("max0", "max1"):
                    u = 1 if kind == "max1" else 0
                    par = (ul + 1) % 2
                    pe.wait_ge(a_read, NB * (unit + 2))
                    for k in range(4):
                        c = P * (4 * u + k)
                        last = pe.transpose(psM[:, P * k:P * (k + 1)], colmax[:, par, c:c + P], ident[:])
                elif kind == "guard":
                    pe.wait_ge(guard_in, unit + 2)
                    last = pe.transpose(psM[0:3 * HH, 0:P], guard[:].rearrange("p a b c -> p (a b c)"), ident[:])
                elif kind == "out":
                    pe.wait_ge(o_read, unit)
                    for s in range(2):
                        last = pe.transpose(psM[:, P * s:P * (s + 1)], outT[:, s, :], ident[:])
                elif kind == "heads":
                    last = pe.transpose(psM[:, 0:P], heads[:], ident[:])
                else:
                    last = pe.matmul(psM[:, 0:D], headsT[:], woT[:], start=True, stop=True)
                last.then_inc(m_done, 1)

            def body(it, first=False, last=False):
                for st in range(4 * NB):
                    ul, jb = divmod(st, NB)
                    b = it * (4 * NB) + st
                    if not (last and st + LEAD >= 4 * NB):
                        al, ja = divmod(st + LEAD, NB)
                        a_tile(b + LEAD, al, ja, it * 2 + al // 2)
                    if not (first and st < 2):
                        pe.wait_ge(e_done, b - 1)
                    if jb == 0:
                        pe.wait_ge(guard_dma, (it * 4 + ul + 1) * 16 * 2)
                    scores(psB[:, st % 2], (ul // 2) % 2, ul % 2, jb).then_inc(b_done, 1)
                    if not (first and st == 0):
                        pu, pj = divmod(st - 1, NB)
                        values(b - 1, pj, pu % 2, it * 4 + pu)
                    e = unit_events(ul, first, last)
                    if jb in e:
                        through_m(e[jb], events_before(it, ul, jb, first, last), it * 4 + ul, ul)

            pe.wait_ge(zero_o, 1)
            for a in range(LEAD):
                ul, ja = divmod(a, NB)
                a_tile(a, ul, ja, 0)
                if a == 17:
                    through_m("max0", 0, -1, -1)
                if a == 18:
                    through_m("max1", 1, -1, -1)
                if a == 20:
                    through_m("guard", 2, -1, -1)
            body(0, first=True)
            with pe.Fori(1, 7) as it:
                body(it)
            body(7, last=True)
            values(8 * 4 * NB - 1, NB - 1, 1, 0)
            n = 20 * 7 + 20 - 3
            through_m("out", n, 32, 0)
            through_m("heads", n + 1, 32, 0)
            through_m("proj", n + 2, 32, 0)

        @block.scalar
        def _(act):
            def exp_tile(b, st, first):
                act.wait_ge(b_done, b + 1)
                if not (first and st < 2):
                    act.wait_ge(pv_done, b - 1)
                act.activation(prob[:, st % 2, :], psB[:, st % 2].rearrange("p a b -> p (a b)"), ACT.Exp)\
                   .then_inc(e_done, 1)

            def rel(n, q):
                if isinstance(n, int) and n < 8:
                    act.wait_ge(rc_first, n + 1)
                else:
                    act.wait_ge(rc_done, n - 7)
                e = rel_exp[:, q % 2].rearrange("p m j -> p (m j)")
                act.activation(e, e, ACT.Exp).then_inc(re_done, 1)

            def first_part(n, c, cm, q):
                act.wait_ge(rr_done, 4 * n + 4)
                if q == 0 and not (isinstance(c, int) and c < 2):
                    act.wait_ge(p_dma[cm % 2], c // 2 * 16)
                act.activation(stage[:, cm % 2, 0, 512 * q:512 * (q + 1)], rel_p[:, q % 2, :], ACT.Copy).then_inc(rp_done, 1)

            def body(it, first=False, last=False):
                for st in range(4 * NB):
                    ul, jb = divmod(st, NB)
                    exp_tile(it * (4 * NB) + st, st, first)
                    if not last and st % 4 == 0:
                        rel(it * 16 + 16 + st // 4, st // 4 % 4)
                    if st % 4 == 1 and not (first and st < 5) and not (last and st >= 5):
                        k = (st - 5) // 4
                        first_part(it * 16 + 16 + k, it * 4 + 4 + k // 4, k // 4 % 4, k % 4)

            for c in range(4):
                rel(4 * c, 0)
                for q in range(4):
                    if q < 3:
                        rel(4 * c + q + 1, q + 1)
                    first_part(4 * c + q, c, c, q)
            body(0, first=True)
            with act.Fori(1, 7) as it:
                body(it)
            body(7, last=True)

        @block.gpsimd
        def _(pool):
            def copy_own(c, par):
                pool.tensor_copy(own[:, par], li[:, :, c:c + 1] if isinstance(c, int) else li[:, :, bass.ds(c, 1)])\
                    .then_inc(own_done, 1)

            def quarter_args(c, n, q, par):
                if not (isinstance(n, int) and n < 2):
                    pool.wait_ge(rs_done, n - 1)
                if q == 0:
                    copy_own(c, par)
                    pool.wait_ge(own_done, c + 1)
                take_waits(pool, pool_waits)
                differences(pool, q, par).then_inc(rc_done, 1)

            def quarter_sum(n, q):
                pool.wait_ge(re_done, n + 1)
                if not (isinstance(n, int) and n < 2):
                    pool.wait_ge(rr_done, 4 * n - 4)
                pool.tensor_tensor(rel_sum[:, q % 2, :], rel_exp[:, q % 2, 0, :], rel_exp[:, q % 2, 1, :],
                                   ALU.add).then_inc(rs_done, 1)

            def quarter_rest(n, q, half):
                pool.wait_ge(rp_done, n + 1)
                if q == 0 and not (isinstance(n, int) and n < 8):
                    pool.wait_ge(p_dma[half], n // 8 * 16)
                pool.tensor_tensor(stage[:, half, 1, 512 * q:512 * (q + 1)], rel_p[:, q % 2, :],
                                   stage[:, half, 0, 512 * q:512 * (q + 1)], ALU.subtract).then_inc(rq_done, 1)

            def chunk(c):
                if c >= 2:
                    quarter_args(c, c * 4, 0, c % 2)
                for q in range(4):
                    if q < 3 and c >= 2:
                        quarter_args(c, c * 4 + q + 1, q + 1, c % 2)
                    quarter_sum(c * 4 + q, q)
                    if q > 0:
                        quarter_rest(c * 4 + q - 1, q - 1, c % 2)
                quarter_rest(c * 4 + 3, 3, c % 2)

            def diagonal(block_no, par):
                g0 = block_no * NG
                src = coef[:, g0:g0 + NG, :] if isinstance(g0, int) else coef[:, bass.ds(g0, NG), :]
                pool.tensor_tensor(diag[:, par].rearrange("p g h i -> p (g h) i"),
                                   src.rearrange("p g h -> p (g h)").unsqueeze(2).broadcast_to([P, NG * H, G]),
                                   dmask[:].unsqueeze(1).broadcast_to([P, NG * H, G]), ALU.mult).then_inc(diag_done, 1)

            def body(it, first=False, last=False):
                for k in range(16):
                    ul, q = divmod(k, 4)
                    blk = it * 2 + ul // 2
                    c = it * 4 + 4 + ul
                    n = it * 16 + 16 + k
                    if not last:
                        quarter_args(c, n, q, ul % 2)
                        quarter_sum(n, q)
                    if not (first and k == 0) and not (last and k > 0):
                        quarter_rest(n - 1, (k - 1) % 4, (k - 1) // 4 % 2)
                    if q == 0 and ul % 2 == 0 and not (first and ul == 0) and not (last and ul == 2):
                        pool.wait_ge(b_done, blk * (2 * NB))
                        diagonal(blk + 1, (ul // 2 + 1) % 2)

            copy_own(0, 0)
            copy_own(1, 1)
            for c in range(4):
                if c == 2:
                    diagonal(0, 0)
                chunk(c)
            diagonal(1, 1)
            body(0, first=True)
            with pool.Fori(1, 7) as it:
                body(it)
            body(7, last=True)

        @block.vector
        def _(dve):
            k = [0]

            def a_max(a, ul, ja):
                dve.wait_ge(a_done, a + 1)
                src, dst = psA[:].rearrange("p a b -> p (a b)"), colmax[:, ul % 2, :]
                if ja == 0:
                    dve.tensor_copy(dst, src).then_inc(a_read, 1)
                else:
                    dve.wait_ge(a_read, a)
                    dve.tensor_tensor(dst, src, dst, ALU.max).then_inc(a_read, 1)

            def recip(n, q, part):
                if part == 0:
                    dve.wait_ge(rs_done, n + 1)
                    if not (isinstance(n, int) and n < 2):
                        dve.wait_ge(rq_done, n - 1)
                cols = slice(P * part, P * (part + 1))
                dve.tensor_scalar(rel_sum[:, q % 2, cols], rel_sum[:, q % 2, cols], 1.0, None, ALU.add).then_inc(r1_done, 1)
                dve.wait_ge(r1_done, 4 * n + part + 1)
                dve.reciprocal(rel_p[:, q % 2, cols], rel_sum[:, q % 2, cols]).then_inc(rr_done, 1)

            def read_m(kind, n, unit, chain):
                def link(ins):
                    chain[0] = chain[0] + 1
                    ins.then_inc(dch, 1)
                    dve.wait_ge(dch, chain[0])

                dve.wait_ge(m_done, n + 1)
                if kind in ("max0", "max1"):
                    u = 1 if kind == "max1" else 0
                    dve.tensor_reduce(rmax[:, 4 * u:4 * u + 4], psM[:].rearrange("p (h j) -> p h j", h=4), AX.X,
                                      ALU.max).then_inc(m_read, 1)
                    if u:
                        dve.wait_ge(m_read, n + 1)
                        link(dve.tensor_scalar(grest[:, 0, :], rmax[:], -1.0, None, ALU.mult))
                        link(dve.tensor_copy(gpart[:, 0, :], grest[:, 0, :]))
                        link(dve.tensor_tensor(grest[:, 1, :], grest[:, 0, :], gpart[:, 0, :], ALU.subtract))
                        link(dve.tensor_copy(gpart[:, 1, :], grest[:, 1, :]))
                        link(dve.tensor_tensor(gpart[:, 2, :], grest[:, 1, :], gpart[:, 1, :], ALU.subtract))
                        dve.tensor_copy(guard[:].rearrange("p hp a pair -> p a pair hp"),
                                        gpart[:].rearrange("p a (pair hp) -> p a pair hp", hp=2)).then_inc(guard_in, 1)
                elif kind == "guard":
                    if not (isinstance(unit, int) and unit < 0):
                        dve.wait_ge(guard_dma, (unit + 1) * 16 * 2)
                    dve.tensor_copy(guardT[:], psM[0:3 * HH, 0:P]).then_inc(m_read, 1)
                elif kind == "out":
                    o = psM[:, 0:2 * P].rearrange("p (h r) -> p h r", r=32)
                    link(dve.reciprocal(rden[:], o[:, :, HD]))
                    half = read_m.half
                    dve.tensor_tensor(heads[:, D // 2 * half:D // 2 * (half + 1)].rearrange("p (h d) -> p h d", d=HD),
                                      o[:, :, 0:HD], rden[:].unsqueeze(2).broadcast_to([P, HH, HD]), ALU.mult)\
                        .then_inc(m_read, 1)
                elif kind == "heads":
                    dve.tensor_copy(headsT[:], psM[:, 0:P]).then_inc(m_read, 1)
                else:
                    blk = (unit - 1) // 2
                    xr = x_res[:, blk, :] if isinstance(blk, int) else x_res[:, bass.ds(blk, 1), :].rearrange("p a d -> p (a d)")
                    if not (isinstance(blk, int) and blk == 0):
                        dve.wait_ge(x1_dma, blk * 16)
                    dve.tensor_tensor(x1[:], psM[:, 0:D], xr, ALU.add).then_inc(m_read, 1)

            def chain_before(it, ul, step, first, last):
                n = 5 if first else it * 24 + 4
                for w in range(ul + 1):
                    for s_, kd in unit_events(w, first, last).items():
                        if w < ul or s_ < step:
                            n = n + {"max1": 5, "out": 1}.get(kd, 0)
                return n

            def take(e, step, it, ul, first, last):
                if step in e:
                    read_m.half = (ul + 1) % 2
                    read_m(e[step], events_before(it, ul, step, first, last), it * 4 + ul,
                           [chain_before(it, ul, step, first, last)])

            def body(it, first=False, last=False):
                for st in range(4 * NB):
                    ul, jb = divmod(st, NB)
                    b = it * (4 * NB) + st
                    if jb == 1 and not (first and ul == 0):
                        dve.wait_ge(pv_done, b - 1)
                        dve.tensor_copy(outT[:].rearrange("p a b -> p (a b)"), psO[:, 0:2 * P]).then_inc(o_read, 1)
                    if not (last and st + LEAD >= 4 * NB):
                        al, ja = divmod(st + LEAD, NB)
                        a_max(b + LEAD, al, ja)
                    if jb > 0:
                        take(unit_events(ul, first, last), jb - 1, it, ul, first, last)
                    if not (first and st < 1) and not (last and st >= 1):
                        k, part = divmod(st - 1, 4)
                        recip(it * 16 + 16 + k, k % 4, part)

            dve.memset(psO[:], 0.0).then_inc(zero_o, 1)
            def first_differences(n):
                dve.wait_ge(own_done, n // 4 + 1)
                if n >= 2:
                    dve.wait_ge(rs_done, n - 1)
                differences(dve, n % 4, n // 4).then_inc(rc_first, 1)

            first_differences(0)
            for n in range(8):
                if n < 7:
                    first_differences(n + 1)
                for part in range(4):
                    recip(n, n % 4, part)
            for a in range(LEAD):
                ul, ja = divmod(a, NB)
                a_max(a, ul, ja)
                for i in (2 * a, 2 * a + 1):
                    if i < 32:
                        recip(8 + i // 4, i // 4 % 4, i % 4)
                if a == 18:
                    read_m("max0", 0, -1, [0])
                if a == 19:
                    read_m("max1", 1, -1, [0])
                if a == 21:
                    read_m("guard", 2, -1, [5])
            body(0, first=True)
            with dve.Fori(1, 7) as it:
                body(it)
            body(7, last=True)
            dve.wait_ge(pv_done, 8 * 4 * NB)
            dve.tensor_copy(outT[:].rearrange("p a b -> p (a b)"), psO[:, 0:2 * P]).then_inc(o_read, 1)
            n = 20 * 7 + 20 - 3
            read_m.half = 1
            read_m("out", n, 32, [chain_before(7, 3, NB, False, True)])
            read_m("heads", n + 1, 32, [0])
            read_m("proj", n + 2, 32, [0])

        @block.sync
        def _(sp):
            def queries(block_no, par):
                t0 = block_no * P
                for hp in range(2):
                    src = io["q_stack"][hp]
                    src = src[:, :, t0:t0 + P] if isinstance(t0, int) else src[:, :, bass.ds(t0, P)]
                    sp.dma_start(qst[64 * hp:64 * hp + GUARD_ROW + 3, par, hp::2, :], src).then_inc(q_dma[par], 16)

            def chunk_out(c, cm):
                sp.wait_ge(rq_done, c * 4 + 4)
                take_waits(sp, sp_waits)
                if isinstance(c, int):
                    there = p_parts[c]
                else:
                    there = p_parts[bass.ds(c, 1)].rearrange("a t p j -> (a t) p j")
                sp.dma_start(there.rearrange("t p j -> p t j"), stage[:, cm % 2]).then_inc(p_dma[cm % 2], 16)

            def chunk_in(c, cm, par):
                sp.wait_ge(p_dma[cm % 2], c // 2 * 16 + 16)
                take_waits(sp, sp_waits)
                for k in range(2):
                    for part, t, times in ((0, 0, 3), (1, 3, 1)):
                        if isinstance(c, int):
                            there = p_parts[c, part]
                        else:
                            there = p_parts[bass.ds(c, 1), part].rearrange("a p j -> (a p) j")
                        w = CH * k + G * t
                        src = there[CH * k:CH * (k + 1), :].rearrange("(i g) j -> i (g j)", i=G)
                        dst = pst[w:w + G * times, par, 4 * (cm % 2):4 * (cm % 2) + 4, :].rearrange("p g j -> p (g j)")
                        if times > 1:
                            src = src.unsqueeze(0).broadcast_to([times, G, CH // G * S])
                        sp.dma_start(dst, src).then_inc(pst_dma[cm], 16)

            def guards(read, ul):
                sp.wait_ge(m_read, read)
                par, half = (ul // 2) % 2, ul % 2
                for hp in range(2):
                    h0 = HH * half + hp
                    r = 64 * hp + GUARD_ROW
                    dst = qst[r:r + 3, par, h0:h0 + HH - 1:2, :]
                    sp.dma_start(dst, guardT[12 * hp:12 * (hp + 1), :]).then_inc(guard_dma, 16)

            def body(it, first=False, last=False):
                for ul in range(4):
                    blk = it * 2 + ul // 2
                    if ul % 2 == 0 and not (first and ul == 0) and not (last and ul == 2):
                        sp.wait_ge(b_done, blk * (2 * NB))
                        take_waits(sp, sp_waits)
                        queries(blk + 1, (ul // 2 + 1) % 2)
                        chunk_in((blk + 1) * 2, (ul + 2) % 4, (ul // 2 + 1) % 2)
                    if not (first and ul == 0) and not (last and ul > 0):
                        chunk_out(it * 4 + ul + 3, (ul + 3) % 4)
                    if ul % 2 == 0 and not (first and ul == 0) and not (last and ul == 2):
                        chunk_in((blk + 1) * 2 + 1, (ul + 3) % 4, (ul // 2 + 1) % 2)
                    if ul % 2 == 0 and not (first and ul == 0):
                        store(blk - 1, events_before(it, ul, 6, first, last) + 1)
                    if not (last and ul == 3):
                        guards(events_before(it, ul, 13, first, last) + 1, (ul + 1) % 4)

            def store(blk, read):
                sp.wait_ge(m_read, read)
                take_waits(sp, sp_waits)
                dst = io["x1"].rearrange("(b p) d -> p b d", p=P)
                dst = dst[:, blk, :] if isinstance(blk, int) else dst[:, bass.ds(blk, 1), :].rearrange("p a d -> p (a d)")
                sp.dma_start(dst, x1[:]).then_inc(x1_dma, 16)

            queries(0, 0)
            queries(1, 1)
            for c in range(4):
                chunk_out(c, c)
                chunk_in(c, c, c // 2)
            guards(3, 0)
            body(0, first=True)
            with sp.Fori(1, 7) as it:
                body(it)
            body(7, last=True)
            store(NB - 1, 20 * 7 + 20 - 3 + 3)
            sp.wait_ge(x1_dma, 16 * NB)


def global_attention(nc, ctx, io):
    sb = lambda n, s, d=F32: ctx.enter_context(nc.sbuf_tensor(n, s, d))
    keep = {
        "x_res": sb("x_res", [P, NB, D]), "ident": sb("ident", [P, P]), "tmask": sb("tmask", [P, 3]),
        "dmask": sb("dmask", [P, G]), "kst": sb("kst", [P, H // 2, S], BF16), "qst": sb("qst", [P, 2, H, P], BF16),
        "v9": sb("v9", [P, NB, H, HD + 1]), "coef": sb("coef", [P, P, H], BF16), "lj": sb("lj", [P, 2, S]),
        "li": sb("li", [P, 2, NC_]), "woT": sb("woT", [P, D]), "zrow": sb("zrow", [3, P], BF16),
        "q_parts": io["q_parts"],
    }
    prepare(nc, io, keep)
    attention(nc, io, keep)


def wait(eng, sem, value):
    if not (isinstance(value, int) and value <= 0):
        eng.wait_ge(sem, value)


def at(ap, dim1):
    if isinstance(dim1, int):
        return ap[:, dim1]
    names = "abcdef"[:len(ap.shape) - 2]
    one = ap[:, bass.ds(dim1, 1)]
    free = " ".join(names)
    return one.rearrange(f"p o {free} -> p (o {names[0]}) {' '.join(names[1:])}")


def local_layers(nc, io):
    with ExitStack() as ctx:
        sb = lambda n, s, d=F32: ctx.enter_context(nc.sbuf_tensor(n, s, d))
        sem = lambda n: ctx.enter_context(nc.semaphore(n))
        wqkv = sb("wqkv", [P, 2, 3 * INNER])
        wo = sb("wo", [P, 2, PAIRS * D])
        w1 = sb("w1", [P, 2, 2 * FF])
        w2 = sb("w2", [P, 2, 3 * D])
        b1_rows = sb("b1_rows", [P, 2, 2 * FF])
        b2_rows = sb("b2_rows", [P, 2, D])
        ln_cols = sb("ln_cols", [P, 2, 2])
        scale_rows = sb("scale_rows", [P, 2, 4 * LD])
        xa = sb("xa", [P, NB + 1, D])
        xm = sb("xm", [P, NB + 1, D])
        rope = sb("rope", [P, NB, 4 * LD])
        mask32 = sb("mask32", [P, 2, 2 * WIN])
        mask = sb("mask", [P, NB, 2 * WIN], BF16)
        ident = sb("ident2", [P, P])
        identb = sb("identb", [P, P], BF16)
        xs_a = sb("xs_a", [P, 2, D])
        xs_f = sb("xs_f", [P, D])
        xsT = sb("xsT", [P, 2, P])
        tab = sb("tab", [P, 2, 4, LD])
        sq = sb("sq", [P, INNER])
        t1 = sb("t1", [P, 2, INNER])
        t2 = sb("t2", [P, 2, INNER])
        ssq = sb("ssq", [P, 2, LH])
        rnq = sb("rnq", [P, 2, LH])
        rnk = sb("rnk", [P, LH])
        kn = sb("kn", [P, INNER])
        qT = sb("qT", [P, 2, PAIRS, P])
        kT = sb("kT", [P, 2, PAIRS, 2, WIN + P])
        vs = sb("vs", [P, 2, INNER])
        v2 = sb("v2", [P, 2, NW, 2, PAIRS, LD])
        mx = sb("mx", [P, LH])
        pr = sb("pr", [P, PAIRS, 2, 2 * WIN])
        den = sb("den", [P, LH])
        rden = sb("rden2", [P, LH])
        prT = sb("prT", [P, PAIRS, P])
        ot = sb("ot", [P, INNER])
        otT = sb("otT", [P, PAIRS, P])
        bn = sb("bn2", [P, 6])
        mv = sb("mv2", [P, 2])
        var = sb("var", [P, 1])
        rstd = sb("rstd2", [P, 1])
        half1 = sb("half1", [P, 2 * LH])
        has_prev = sb("has_prev", [P, NB])
        prev = sb("prev", [P, 1])
        xn = sb("xn2", [P, D])
        xnT = sb("xnT2", [P, P])
        hs = sb("hs", [P, 2, FF])
        gs = sb("gs", [P, FF])
        gT = sb("gT", [P, 3, P])
        xmb = sb("xmb", [P, D])
        bn16 = sb("bn16", [P, NB, 6])
        mv16 = sb("mv16", [P, NB, 2])
        rs16 = sb("rs16", [P, NB])
        R = [ctx.enter_context(nc.psum_tensor(f"R{i}", [P, 2, 512], F32)) for i in range(4)]
        flat = [r[:].rearrange("p a b -> p (a b)") for r in R]

        names = """init_dma init_dve init_pool w_dma xs_f_dma xT_done xT_ready q_done k_done v_done sq_done
            tq_done tk_done ssq_done clamp_done rn_done add_done kn_done qT_done kT_done qT_ready kT_ready
            s_done mx_done sub_done scaled_done exp_done sum_done rden_done pT_done pT_ready pv2_done o_ready
            oT_done oT_ready wo_done x2_done st_done lnv_done eps_done rstd_done xn_done xnT_done xnT_ready h_done
            hb_done gelu_done g_done gT_done gT_ready w2_done xmb_done x3_done v_ready tab_done prev_done q_added out_dma
            pool_taken dve_taken sp_taken""".split()
        m = {n: sem(n) for n in names}
        xs_a_dma = [sem("xs_a_dma0"), sem("xs_a_dma1")]
        v2_dma = [sem("v2_dma0"), sem("v2_dma1")]

        def load(sp, l, parts=(0, 1, 2)):
            par = l % 2
            def vec(name, lo, n):
                return io[name][l:l + 1, lo:lo + n] if isinstance(l, int) else io[name][bass.ds(l, 1), lo:lo + n]
            def mat(name, r0, r1):
                a = io[name]
                return a[l, r0:r1, :] if isinstance(l, int) else a[bass.ds(l, 1), r0:r1, :].rearrange("a r c -> (a r) c")
            def to(tile, lo, hi, rows=P):
                if isinstance(l, int):
                    return tile[0:rows, par, lo:hi]
                return tile[0:rows, bass.ds(par, 1), lo:hi].rearrange("p a f -> p (a f)")
            wide = lambda v: v.rearrange("a f -> (a f)").partition_broadcast(P)
            hd = LD // 2
            wqkv_part = lambda i: (to(wqkv, INNER * i, INNER * (i + 1)),
                                   io["Wqkv"][l, :, INNER * i:INNER * (i + 1)] if isinstance(l, int) else
                                   io["Wqkv"][bass.ds(l, 1), :, INNER * i:INNER * (i + 1)].rearrange("a r c -> (a r) c"))
            scales = [
                (to(scale_rows, 2 * LD * i + o, 2 * LD * i + o + w), wide(vec(name, lo, w)))
                for i, name in enumerate(("q_scale", "k_scale"))
                for o, lo, w in ((0, 0, LD), (LD, hd, hd), (LD + hd, 0, hd))
            ]
            jobs = (
                (wqkv_part(0),
                 (to(w2, 0, 2 * D).rearrange("p (c n) -> p c n", n=D),
                  mat("W2", 0, 2 * P).rearrange("(c p) n -> p c n", p=P)),
                 (to(w2, 2 * D, 3 * D, FF - 2 * P), mat("W2", 2 * P, FF)),
                 (to(b1_rows, 0, 2 * FF), wide(vec("b1", 0, 2 * FF))),
                 (to(b2_rows, 0, D), wide(vec("b2", 0, D)))),
                (wqkv_part(1),
                 (to(w1, 0, 2 * FF), mat("W1", 0, D)),
                 (to(ln_cols, 0, 1), vec("ln_g", 0, D).rearrange("a f -> f a")),
                 (to(ln_cols, 1, 2), vec("ln_b", 0, D).rearrange("a f -> f a")),
                 *scales[0:2]),
                (wqkv_part(2),
                 (to(wo, 0, PAIRS * D).rearrange("p (c n) -> p c n", n=D),
                  mat("Wo2", 0, INNER).rearrange("(c p) n -> p c n", p=P)),
                 *scales[2:6]),
            )
            assert sum(len(part) for part in jobs) == NWL
            for part in parts:
                for dst, src in jobs[part]:
                    sp.dma_start(dst, src).then_inc(m["w_dma"], 16)

        with nc.Block() as block:
            @block.sync
            def _(sp):
                for dst, src in ((xm[:, 1:NB + 1, :], io["x1"].rearrange("(b p) d -> p b d", p=P)),
                                 (rope[:], io["rope"]), (mask32[:], io["mask"]), (ident[:], io["ident"])):
                    sp.dma_start(dst, src).then_inc(m["init_dma"], 16)
                load(sp, 0)

            @block.gpsimd
            def _(pool):
                n = 0
                for tile, value in ((half1[:], -0.5), (vs[:], 0.0), (v2[:], 0.0), (kT[:], 0.0)):
                    pool.memset(tile, value).then_inc(m["init_pool"], 1)
                    n += 1
                pool.wait_ge(m["init_dve"], 2)
                pool.wait_ge(m["init_pool"], n)
                pool.tensor_scalar(mv16[:, :, 1], mv16[:, :, 1], 1e-5, None, ALU.add).then_inc(m["init_pool"], 1)
                pool.wait_ge(m["init_pool"], n + 1)
                pool.tensor_tensor(rs16[:], mv16[:, :, 1], half1[:, 0:NB], ALU.pow).then_inc(m["init_pool"], 1)

            @block.vector
            def _(dve):
                dve.wait_ge(m["init_dma"], 16 * 4)
                for b in range(NB):
                    last = dve.bn_stats(bn16[:, b, :], xm[:, b + 1, :])
                last.then_inc(m["init_dve"], 1)
                dve.wait_ge(m["init_dve"], 1)
                for b in range(NB):
                    last = dve.bn_aggr(mv16[:, b, :], bn16[:, b, :])
                last.then_inc(m["init_dve"], 1)
                dve.memset(xa[:, 0, :], 0.0)
                dve.memset(xm[:, 0, :], 0.0)
                dve.memset(has_prev[:, 0:1], 0.0)
                dve.memset(has_prev[:, 1:NB], 1.0)
                dve.tensor_copy(identb[:], ident[:])
                dve.tensor_copy(mask[:, 0, :], mask32[:, 0, :])
                dve.tensor_copy(mask[:, 1:NB, :], mask32[:, 1:2, :].broadcast_to([P, NB - 1, 2 * WIN]))
                dve.wait_ge(m["init_pool"], 6)
                dve.tensor_tensor(xa[:, 1:NB + 1, :], xm[:, 1:NB + 1, :], mv16[:, :, 0:1].broadcast_to([P, NB, D]),
                                  ALU.subtract).then_inc(m["init_dve"], 1)
                dve.wait_ge(m["init_dve"], 3)
                dve.tensor_tensor(xa[:, 1:NB + 1, :], xa[:, 1:NB + 1, :], rs16[:].unsqueeze(2).broadcast_to([P, NB, D]),
                                  ALU.mult).then_inc(m["x3_done"], NB)

        def wp(n):
            return (n // NB) % 2

        def steps(eng, step):
            for s in range(4):
                step(s, s % 2)
            with eng.Fori(2, NT // 2 - 1) as i:
                step(i * 2, 0)
                step(i * 2 + 1, 1)
            for s in range(NT - 2, NT + 3):
                step(s, s % 2)

        def stages(s):
            if isinstance(s, int):
                return s < NT, 1 <= s <= NT, 2 <= s <= NT + 1, 3 <= s
            return True, True, True, True

        def slot(tile, n, k=0):
            if isinstance(n, int):
                return tile[:, n + k, :]
            return tile[:, bass.ds(n + k, 1), :].rearrange("p a f -> p (a f)")

        with nc.Block() as block:
            @block.tensor
            def _(pe):
                def turn_x(n, par):
                    wait(pe, xs_a_dma[par], (n // 2 + 1) * 48)
                    pe.transpose(flat[1][:, 512:512 + P], xs_a[:, par, :], ident[:]).then_inc(m["xT_done"], 1)

                def project(n, par, which, bank, done):
                    w = at(wqkv, wp(n))
                    for c in range(2):
                        last = pe.matmul(R[bank][:, c, :], xsT[:, par, :],
                                         w[:, INNER * which + 512 * c:INNER * which + 512 * (c + 1)], start=True, stop=True)
                    last.then_inc(m[done], 1)

                def step(s, par):
                    a, b, o, c = stages(s)
                    n, u, k = s - 1, s - 2, s - 3
                    if a:
                        if isinstance(s, int) and s == 0:
                            turn_x(0, 0)
                        wait(pe, m["w_dma"], (s // NB + 1) * (16 * NWL))
                        wait(pe, m["xT_ready"], s + 1)
                        wait(pe, m["x3_done"], s - 3 + NB)
                        project(s, par, 0, 0, "q_done")
                    if o:
                        wait(pe, m["exp_done"], u + 1)
                        wait(pe, m["tk_done"], min(u + 2, NT) if isinstance(u, int) else u + 2)
                        wait(pe, m["sq_done"], 2 * min(u + 2, NT) if isinstance(u, int) else 2 * u + 4)
                        for i in range(PAIRS):
                            last = pe.transpose(flat[1][:, P * i:P * (i + 1)], pr[:, i].rearrange("p a b -> p (a b)"), ident[:])
                        last.then_inc(m["pT_done"], 1)
                    if a:
                        wait(pe, m["oT_ready"], s - 2)
                        project(s, par, 2, 2, "v_done")
                    if o:
                        wait(pe, m["pT_ready"], u + 1)
                        wait(pe, v2_dma[par], (u // 2 + 1) * 160)
                        wait(pe, m["x2_done"], u)
                        for i in range(PAIRS):
                            for w in range(NW):
                                last = pe.matmul(flat[3][WIN * w:WIN * (w + 1), P * i:P * (i + 1)],
                                                 prT[:, i, WIN * w:WIN * (w + 1)], v2[:, par, w, :, i, :], start=True,
                                                 stop=True, skip_group_check=True)
                        last.then_inc(m["pv2_done"], 1)
                    if a and (not isinstance(s, int) or s + 1 < NT):
                        if isinstance(s, int) and s == 1:
                            wait(pe, m["tk_done"], 1)
                            wait(pe, m["sq_done"], 2)
                        turn_x(s + 1, 1 - par)
                    if b:
                        wait(pe, m["kn_done"], n + 1)
                        if a:
                            wait(pe, m["v_ready"], s + 1)
                        else:
                            wait(pe, m["oT_ready"], n - 1)
                        for i in range(PAIRS):
                            last = pe.transpose(flat[2][:, P * i:P * (i + 1)], kn[:, P * i:P * (i + 1)], ident[:])
                        last.then_inc(m["kT_done"], 1)
                    if c:
                        wait(pe, m["xn_done"], k + 1)
                        pe.transpose(flat[1][:, 0:P], xn[:], ident[:]).then_inc(m["xnT_done"], 1)
                    if c:
                        wait(pe, m["xnT_ready"], k + 1)
                        if a:
                            wait(pe, m["tq_done"], s + 1)
                            wait(pe, m["sq_done"], 2 * s + 1)
                        else:
                            wait(pe, m["x3_done"], k + NB)
                        w = slot(w1, wp(k))
                        for i in range(2):
                            last = pe.matmul(R[0][:, i, 0:FF], xnT[:], w[:, FF * i:FF * (i + 1)], start=True, stop=True)
                        last.then_inc(m["h_done"], 1)
                    if a:
                        wait(pe, m["q_added"], s + 1)
                        if c:
                            wait(pe, m["xnT_ready"], k + 1)
                        wait(pe, m["xT_ready"], min(s + 2, NT) if isinstance(s, int) else s + 2)
                        for i in range(PAIRS):
                            last = pe.transpose(flat[1][:, P * i:P * (i + 1)], t1[:, 0, P * i:P * (i + 1)], ident[:])
                        last.then_inc(m["qT_done"], 1)
                    if b:
                        wait(pe, m["qT_ready"], n + 1)
                        wait(pe, m["kT_ready"], n + 1)
                        wait(pe, m["o_ready"], n)
                        mk = slot(mask, n % NB)
                        for half in range(2):
                            pe.matmul(R[3][:, half, :], identb[:], mk.unsqueeze(1).broadcast_to([P, PAIRS, 2 * WIN]),
                                      start=True, stop=False, skip_group_check=True)
                        for i in range(PAIRS):
                            for w in range(NW):
                                last = pe.matmul(flat[3][WIN * w:WIN * (w + 1), P * i:P * (i + 1)],
                                                 qT[:, 1 - par, i, WIN * w:WIN * (w + 1)],
                                                 kT[:, 1 - par, i, :, WIN * w:WIN * (w + 2)],
                                                 start=False, stop=True, skip_group_check=True)
                        last.then_inc(m["s_done"], 1)
                    if a:
                        wait(pe, m["qT_ready"], s + 1)
                        project(s, par, 1, 1, "k_done")
                    if c:
                        wait(pe, m["g_done"], k + 1)
                        for i, (lo, w) in enumerate(FC):
                            last = pe.transpose(flat[0][0:w, P * i:P * (i + 1)], gs[:, lo:lo + w], ident[:])
                        last.then_inc(m["gT_done"], 1)
                    if o:
                        wait(pe, m["o_ready"], u + 1)
                        if b:
                            wait(pe, m["kT_ready"], n + 1)
                        else:
                            wait(pe, m["oT_ready"], u)
                        for i in range(PAIRS):
                            last = pe.transpose(flat[2][:, P * i:P * (i + 1)], ot[:, P * i:P * (i + 1)], ident[:])
                        last.then_inc(m["oT_done"], 1)
                    if c:
                        wait(pe, m["gT_ready"], k + 1)
                        w = slot(w2, wp(k))
                        for i, (lo, r) in enumerate(FC):
                            last = pe.matmul(flat[0][:, 512:512 + D], gT[0:r, i, :], w[0:r, D * i:D * (i + 1)],
                                             start=(i == 0), stop=(i == 2))
                        last.then_inc(m["w2_done"], 1)
                    if o:
                        wait(pe, m["oT_ready"], u + 1)
                        if b:
                            wait(pe, m["sub_done"], n + 1)
                        w = slot(wo, wp(u))
                        for i in range(PAIRS):
                            last = pe.matmul(flat[3][:, 0:D], otT[:, i, :], w[:, D * i:D * (i + 1)],
                                             start=(i == 0), stop=(i == PAIRS - 1))
                        last.then_inc(m["wo_done"], 1)

                steps(pe, step)

            @block.scalar
            def _(act):
                def copy(dst, src, ready):
                    act.activation(dst, src, ACT.Copy).then_inc(m[ready], 1)

                def xT_out(n, par):
                    wait(act, m["xT_done"], n + 1)
                    copy(xsT[:, par, :], flat[1][:, 512:512 + P], "xT_ready")

                def step(s, par):
                    a, b, o, c = stages(s)
                    n, u, k = s - 1, s - 2, s - 3
                    if isinstance(s, int) and s == 0:
                        xT_out(0, 0)
                    if o:
                        wait(act, m["pT_done"], u + 1)
                        wait(act, m["pv2_done"], u)
                        copy(prT[:].rearrange("p a b -> p (a b)"), flat[1], "pT_ready")
                    if a:
                        wait(act, m["tq_done"], s + 1)
                        wait(act, m["ssq_done"], 2 * s)
                        act.activation(sq[:], flat[0], ACT.Square).then_inc(m["sq_done"], 1)
                    if a:
                        wait(act, m["v_done"], s + 1)
                        wait(act, v2_dma[1 - par], (s + 1) // 2 * 160)
                        act.activation(vs[:, par, :].rearrange("p (hp i d) -> p hp i d", hp=2, d=LD),
                                       flat[2].rearrange("p (i hp d) -> p hp i d", hp=2, d=LD), ACT.Copy)\
                           .then_inc(m["v_ready"], 1)
                    if a and (not isinstance(s, int) or s + 1 < NT):
                        xT_out(s + 1, 1 - par)
                    if b:
                        wait(act, m["kT_done"], n + 1)
                        wait(act, m["s_done"], n)
                        keys = flat[2].rearrange("p (a b) -> p a b", b=P)
                        for hp in range(2):
                            r = slice(LD * hp, LD * (hp + 1))
                            act.activation(kT[r, 1 - par, :, hp, WIN:WIN + P], keys[r], ACT.Copy)
                        wait(act, m["prev_done"], n + 1)
                        for hp in range(2):
                            r = slice(LD * hp, LD * (hp + 1))
                            last = act.activation(kT[r, par, :, hp, 0:WIN], keys[r, :, P - WIN:P], ACT.Copy,
                                                  scale=prev[r, 0:1])
                        last.then_inc(m["kT_ready"], 1)
                    if a:
                        wait(act, m["qT_done"], s + 1)
                        wait(act, m["s_done"], s - 1)
                        copy(qT[:, par].rearrange("p a b -> p (a b)"), flat[1], "qT_ready")
                    if c:
                        wait(act, m["hb_done"], k + 1)
                        act.activation(hs[:, 1, :], hs[:, 1, :], ACT.Gelu).then_inc(m["gelu_done"], 1)
                    if a:
                        wait(act, m["k_done"], s + 1)
                        wait(act, m["ssq_done"], 2 * s + 1)
                        act.activation(sq[:], flat[1], ACT.Square).then_inc(m["sq_done"], 1)
                    if c:
                        wait(act, m["gT_done"], k + 1)
                        wait(act, m["w2_done"], k)
                        act.activation(gT[:, 0:2, :], flat[0][:, 0:2 * P].rearrange("p (a b) -> p a b", b=P), ACT.Copy)
                        w = FC[2][1]
                        act.activation(gT[0:w, 2, :], flat[0][0:w, 2 * P:3 * P], ACT.Copy).then_inc(m["gT_ready"], 1)
                    if o:
                        wait(act, m["oT_done"], u + 1)
                        wait(act, m["wo_done"], u)
                        copy(otT[:].rearrange("p a b -> p (a b)"), flat[2], "oT_ready")
                    if b:
                        wait(act, m["scaled_done"], n + 1)
                        p = pr[:].rearrange("p a b c -> p (a b c)")
                        act.activation(p, p, ACT.Exp, scale=QK_SCALE).then_inc(m["exp_done"], 1)

                steps(act, step)

            @block.gpsimd
            def _(pool):
                def table(n, par):
                    wait(pool, m["w_dma"], (n // NB + 1) * (16 * NWL))
                    wait(pool, m["tk_done"], n - 1)
                    pool.tensor_tensor(tab[:, par].rearrange("p a b -> p (a b)"), slot(rope, n % NB),
                                       slot(scale_rows, wp(n)), ALU.mult).then_inc(m["tab_done"], 1)

                def root(i, n, dst):
                    wait(pool, m["ssq_done"], 2 * n + 1 + i)
                    take_waits(pool, m["pool_taken"])
                    pool.tensor_scalar(ssq[:, i, :], ssq[:, i, :], 1e-24, None, ALU.max).then_inc(m["clamp_done"], 1)
                    wait(pool, m["clamp_done"], 2 * n + 1 + i)
                    pool.tensor_tensor(dst, ssq[:, i, :], half1[:, 0:LH], ALU.pow).then_inc(m["rn_done"], 1)

                def step(s, par):
                    a, b, o, c = stages(s)
                    n, u, k = s - 1, s - 2, s - 3
                    if isinstance(s, int) and s == 0:
                        table(0, 0)
                    if b:
                        wait(pool, m["kT_ready"], n)
                        flag = has_prev[:, s % NB:s % NB + 1] if isinstance(s, int) else has_prev[:, bass.ds(s % NB, 1)]
                        pool.tensor_copy(prev[:], flag).then_inc(m["prev_done"], 1)
                        wait(pool, m["tk_done"], n + 1)
                        pool.tensor_tensor(t1[:, 1, :], t1[:, 1, :], t2[:, 1, :], ALU.add).then_inc(m["add_done"], 1)
                        root(1, n, rnk[:])
                        wait(pool, m["add_done"], n + 1)
                        wait(pool, m["rn_done"], 2 * n + 2)
                        wait(pool, m["kT_done"], n)
                        pool.tensor_tensor(kn[:].rearrange("p (h d) -> p h d", d=LD),
                                           t1[:, 1, :].rearrange("p (h d) -> p h d", d=LD),
                                           rnk[:].unsqueeze(2).broadcast_to([P, LH, LD]), ALU.mult)\
                            .then_inc(m["kn_done"], 1)
                    if c:
                        wait(pool, m["lnv_done"], k + 1)
                        take_waits(pool, m["pool_taken"])
                        pool.tensor_scalar(var[:], mv[:, 1:2], 1e-5, None, ALU.add).then_inc(m["eps_done"], 1)
                        wait(pool, m["eps_done"], k + 1)
                        pool.tensor_tensor(rstd[:], var[:], half1[:, 0:1], ALU.pow).then_inc(m["rstd_done"], 1)
                        wait(pool, m["x2_done"], k + 1)
                        wait(pool, m["x3_done"], k + NB)
                        pool.tensor_tensor(xmb[:], slot(xm, k % NB, 1), slot(b2_rows, wp(k)), ALU.add)\
                            .then_inc(m["xmb_done"], 1)
                    if a:
                        wait(pool, m["tq_done"], s + 1)
                        pool.tensor_tensor(t1[:, 0, :], t1[:, 0, :], t2[:, 0, :], ALU.add).then_inc(m["q_added"], 1)
                        root(0, s, rnq[:, par, :])
                        if not isinstance(s, int) or s + 1 < NT:
                            table(s + 1, 1 - par)
                    if b:
                        wait(pool, m["sub_done"], n + 1)
                        wait(pool, m["rn_done"], 2 * n + 1)
                        p = pr[:].rearrange("p i a k -> p (i a) k")
                        pool.tensor_tensor(p, p, rnq[:, 1 - par, :].unsqueeze(2).broadcast_to([P, LH, 2 * WIN]),
                                           ALU.mult).then_inc(m["scaled_done"], 1)

                steps(pool, step)

            @block.vector
            def _(dve):
                def rotate(s, par, i, bank, done):
                    wait(dve, *((m["q_done"], s + 1) if i == 0 else (m["sq_done"], 2 * s + 2)))
                    wait(dve, m["tab_done"], s + 1)
                    wait(dve, m["qT_done" if i == 0 else "kn_done"], s)
                    q = flat[bank].rearrange("p (h d) -> p h d", d=LD)
                    o1 = t1[:, i, :].rearrange("p (h d) -> p h d", d=LD)
                    o2 = t2[:, i, :].rearrange("p (h d) -> p h d", d=LD)
                    tb = lambda row, lo, hi: tab[:, par, row, lo:hi].unsqueeze(1).broadcast_to([P, LH, hi - lo])
                    dve.tensor_tensor(o1, q, tb(2 * i, 0, LD), ALU.mult)
                    hd = LD // 2
                    dve.tensor_tensor(o2[:, :, 0:hd], q[:, :, hd:LD], tb(2 * i + 1, 0, hd), ALU.mult)
                    dve.tensor_tensor(o2[:, :, hd:LD], q[:, :, 0:hd], tb(2 * i + 1, hd, LD), ALU.mult).then_inc(m[done], 1)

                def squares(s, i):
                    wait(dve, m["sq_done"], 2 * s + 1 + i)
                    wait(dve, m["rn_done"], 2 * s - 1 + i)
                    dve.tensor_reduce(ssq[:, i, :], sq[:].rearrange("p (h d) -> p h d", d=LD), AX.X, ALU.add)\
                       .then_inc(m["ssq_done"], 1)

                def step(s, par):
                    a, b, o, c = stages(s)
                    n, u, k = s - 1, s - 2, s - 3
                    if o:
                        wait(dve, m["exp_done"], u + 1)
                        dve.tensor_reduce(den[:], pr[:].rearrange("p i a k -> p (i a) k"), AX.X, ALU.add).then_inc(m["sum_done"], 1)
                        wait(dve, m["sum_done"], u + 1)
                        wait(dve, m["o_ready"], u)
                        dve.reciprocal(rden[:], den[:]).then_inc(m["rden_done"], 1)
                    if a:
                        rotate(s, par, 0, 0, "tq_done")
                    if c:
                        wait(dve, m["xs_f_dma"], (k + 1) * 48)
                        dve.bn_stats(bn[:], xs_f[:]).then_inc(m["st_done"], 1)
                        wait(dve, m["st_done"], k + 1)
                        wait(dve, m["rstd_done"], k)
                        take_waits(dve, m["dve_taken"])
                        dve.bn_aggr(mv[:], bn[:]).then_inc(m["lnv_done"], 1)
                    if a:
                        squares(s, 0)
                    if c:
                        wait(dve, m["rstd_done"], k + 1)
                        wait(dve, m["lnv_done"], k + 1)
                        wait(dve, m["xnT_done"], k)
                        dve.tensor_scalar(xn[:], xs_f[:], mv[:, 0:1], rstd[:, 0:1], ALU.subtract, ALU.mult)\
                           .then_inc(m["xn_done"], 1)
                    if o:
                        wait(dve, m["pv2_done"], u + 1)
                        wait(dve, m["rden_done"], u + 1)
                        wait(dve, m["oT_done"], u)
                        dve.tensor_tensor(ot[:].rearrange("p (h d) -> p h d", d=LD), flat[3].rearrange("p (h d) -> p h d", d=LD),
                                          rden[:].unsqueeze(2).broadcast_to([P, LH, LD]), ALU.mult).then_inc(m["o_ready"], 1)
                    if c:
                        wait(dve, m["xnT_done"], k + 1)
                        wait(dve, m["h_done"], k)
                        l = slot(ln_cols, wp(k))
                        dve.tensor_scalar(xnT[:], flat[1][:, 0:P], l[:, 0:1], l[:, 1:2], ALU.mult, ALU.add)\
                           .then_inc(m["xnT_ready"], 1)
                        wait(dve, m["h_done"], k + 1)
                        wait(dve, m["g_done"], k)
                        dve.tensor_tensor(hs[:], R[0][:, :, 0:FF], slot(b1_rows, wp(k)).rearrange("p (a f) -> p a f", a=2),
                                          ALU.add).then_inc(m["hb_done"], 1)
                    if c:
                        wait(dve, m["gelu_done"], k + 1)
                        wait(dve, m["gT_done"], k)
                        dve.tensor_tensor(gs[:], hs[:, 0, :], hs[:, 1, :], ALU.mult).then_inc(m["g_done"], 1)
                    if b:
                        wait(dve, m["s_done"], n + 1)
                        dve.tensor_reduce(mx[:], flat[3].rearrange("p (h k) -> p h k", k=2 * WIN), AX.X, ALU.max)\
                           .then_inc(m["mx_done"], 1)
                        wait(dve, m["mx_done"], n + 1)
                        wait(dve, m["pT_done"], n)
                        dve.tensor_tensor(pr[:].rearrange("p i a k -> p (i a) k"),
                                          flat[3].rearrange("p (h k) -> p h k", k=2 * WIN),
                                          mx[:].unsqueeze(2).broadcast_to([P, LH, 2 * WIN]), ALU.subtract)\
                           .then_inc(m["sub_done"], 1)
                    if a:
                        rotate(s, par, 1, 1, "tk_done")
                    if c:
                        wait(dve, m["w2_done"], k + 1)
                        wait(dve, m["xmb_done"], k + 1)
                        for q in range(2):
                            if not isinstance(k, int) or k + 2 - q >= 2:
                                dve.wait_ge(xs_a_dma[q], ((k + 2 - q) // 2) * 48)
                        dve.tensor_tensor(slot(xa, k % NB, 1), flat[0][:, 512:512 + D], xmb[:], ALU.add)\
                           .then_inc(m["x3_done"], 1)
                    if a:
                        squares(s, 1)
                    if o:
                        wait(dve, m["wo_done"], u + 1)
                        dve.tensor_tensor(slot(xm, u % NB, 1), flat[3][:, 0:D], slot(xa, u % NB, 1), ALU.add)\
                           .then_inc(m["x2_done"], 1)

                steps(dve, step)

            @block.sync
            def _(sp):
                def shift(dst, src, n, done):
                    b = n % NB
                    take_waits(sp, m["sp_taken"])
                    if isinstance(n, int):
                        own, before = src[:, b + 1, :], src[P - 1:P, b, D // 2:D]
                    else:
                        own = src[:, bass.ds(b + 1, 1), :].rearrange("p a f -> p (a f)")
                        before = src[P - 1:P, bass.ds(b, 1), D // 2:D].rearrange("p a f -> p (a f)")
                    sp.dma_start(dst[:, 0:D // 2], own[:, 0:D // 2]).then_inc(done, 16)
                    sp.dma_start(dst[1:P, D // 2:D], own[0:P - 1, D // 2:D]).then_inc(done, 16)
                    sp.dma_start(dst[0:1, D // 2:D], before).then_inc(done, 16)

                def shift_a(n, par):
                    wait(sp, m["x3_done"], n + 1)
                    wait(sp, m["xT_done"], n - 1)
                    shift(xs_a[:, par, :], xa, n, xs_a_dma[par])

                def step(s, par, also=None):
                    a, b, o, c = stages(s)
                    u = s - 2
                    if a and (not isinstance(s, int) or s + 1 < NT):
                        shift_a(s + 1, 1 - par)
                    if a:
                        wait(sp, m["v_ready"], s + 1)
                        take_waits(sp, m["sp_taken"])
                        wait(sp, m["pv2_done"], s - 1)
                        for hp in range(2):
                            cols = slice(PAIRS * LD * hp, PAIRS * LD * (hp + 1))
                            r = 2 * WIN * hp
                            v = lambda lo, hi, w: v2[r + lo:r + hi, par, w, hp, :, :].rearrange("p i d -> p (i d)")
                            sp.dma_start(v(0, WIN, 0), vs[P - WIN:P, 1 - par, cols]).then_inc(v2_dma[par], 16)
                            sp.dma_start(v(WIN, 2 * WIN, 0), vs[0:WIN, par, cols]).then_inc(v2_dma[par], 16)
                            for w in range(1, NW):
                                sp.dma_start(v(0, 2 * WIN, w), vs[WIN * (w - 1):WIN * (w + 1), par, cols])\
                                  .then_inc(v2_dma[par], 16)
                    if also:
                        also()
                    if o:
                        wait(sp, m["x2_done"], u + 1)
                        take_waits(sp, m["sp_taken"])
                        wait(sp, m["xn_done"], u)
                        shift(xs_f, xm, u, m["xs_f_dma"])

                def pair(i, also0=None, also1=None):
                    step(i * 2, 0, also0)
                    step(i * 2 + 1, 1, also1)

                half = NB // 2
                shift_a(0, 0)
                for s in range(4):
                    step(s, s % 2)
                    if s == 1:
                        load(sp, 1)
                with sp.Fori(2, half) as i:
                    pair(i)
                with sp.Fori(1, LAYERS - 1) as l:
                    def first_part():
                        sp.wait_ge(m["x3_done"], NB * l + NB)
                        take_waits(sp, m["sp_taken"])
                        load(sp, l + 1, (0,))

                    pair(l * half)
                    pair(l * half + 1, None, first_part)
                    pair(l * half + 2, lambda: load(sp, l + 1, (1,)), lambda: load(sp, l + 1, (2,)))
                    with sp.Fori(3, half) as i:
                        pair(l * half + i)
                with sp.Fori((LAYERS - 1) * half, LAYERS * half - 1) as i:
                    pair(i)
                for s in range(NT - 2, NT + 3):
                    step(s, s % 2)

        with nc.Block() as block:
            @block.sync
            def _(sp):
                sp.dma_start(xm[:, 1:NB + 1, :], io["x1"].rearrange("(b p) d -> p b d", p=P)).then_inc(m["init_dma"], 16)
                sp.wait_ge(m["init_dve"], 4)
                sp.dma_start(io["out"].rearrange("a (b p) d -> p (a b) d", p=P), xa[:, 1:NB + 1, :]).then_inc(m["out_dma"], 16)
                sp.wait_ge(m["out_dma"], 16)

            @block.vector
            def _(dve):
                dve.wait_ge(m["init_dma"], 16 * 5)
                dve.tensor_tensor(xa[:, 1:NB + 1, :], xa[:, 1:NB + 1, :], xm[:, 1:NB + 1, :], ALU.add)\
                   .then_inc(m["init_dve"], 1)


def global_constants():
    r = np.arange(P)
    term = r % 64 // G
    return {
        "ident": np.eye(P, dtype=np.float32),
        "tmask": np.stack([(term == 0) | (term == 3), term == 1, term == 2], 1).astype(np.float32),
        "dmask": (r[:, None] % G == np.arange(G)[None]).astype(np.float32),
    }


def local_constants():
    f = np.float32
    half = np.arange(0, LD, 2, dtype=f)
    freqs = np.arange(S, dtype=f)[:, None] * (f(1.0) / f(10000.0) ** (half / f(LD)))[None, :]
    freqs = np.concatenate([freqs, freqs], -1)
    base = (half + f(0.4 * LD)) / f(1.4 * LD)
    power = (np.arange(S, dtype=f) - f(S // 2)) / f(WIN // 2)
    scale = base[None, :] ** power[:, None]
    scale = np.concatenate([scale, scale], -1)
    cos, sin = np.cos(freqs), np.sin(freqs)
    sign = np.where(np.arange(LD) < LD // 2, f(-1), f(1))[None, :]
    inv = f(1.0) / scale
    rope = np.stack([cos * scale, sin * scale * sign, cos * inv, sin * inv * sign], 1).astype(f)
    rope = rope.reshape(NB, P, 4 * LD).transpose(1, 0, 2)
    q = np.arange(P) % WIN
    key = np.arange(2 * WIN) - WIN
    banned = (q[:, None] < key[None]) | (q[:, None] > key[None] + WIN)
    first = banned | ((np.arange(P) < WIN)[:, None] & (key < 0)[None])
    return {"rope": np.ascontiguousarray(rope),
            "mask": np.stack([np.where(b, f(-1e25), f(0)) for b in (first, banned)], 1).astype(f)}


def program(nc, x, wq, bq, wk, bk, wv, bv, wo, bo, rel_w, rel_b, logical_bias, gate_w, gate_b,
            wqkv, q_scale, k_scale, wo2, ln_g, ln_b, w1, b1, w2, b2, ident, tmask, dmask, rope, mask, out):
    io = {
        "x": x, "Wq": wq, "bq": bq, "Wk": wk, "bk": bk, "Wv": wv, "bv": bv, "Wo": wo, "bo": bo, "rel_W": rel_w,
        "rel_b": rel_b, "logical_bias": logical_bias, "gate_W": gate_w, "gate_b": gate_b, "Wqkv": wqkv,
        "q_scale": q_scale, "k_scale": k_scale, "Wo2": wo2, "ln_g": ln_g, "ln_b": ln_b, "W1": w1, "b1": b1,
        "W2": w2, "b2": b2, "ident": ident, "tmask": tmask, "dmask": dmask, "rope": rope, "mask": mask, "out": out,
        "q_parts": nc.dram_tensor("q_parts", [3, D, S], BF16, kind="Internal").ap(),
        "q_stack": nc.dram_tensor("q_stack", [2, GUARD_ROW + 3, H // 2, S], BF16, kind="Internal").ap(),
        "k_parts": nc.dram_tensor("k_parts", [3, D, S], BF16, kind="Internal").ap(),
        "p_parts": nc.dram_tensor("p_parts", [NC_, 2, P, S], FP16, kind="Internal").ap(),
        "x1": nc.dram_tensor("x1", [S, D], F32, kind="Internal").ap(),
    }
    with ExitStack() as ctx:
        global_attention(nc, ctx, io)
    local_layers(nc, io)


_INS = [f"L0_attn_{n}" for n in ("hidden_states", "Wq", "bq", "Wk", "bk", "Wv", "bv", "Wo", "bo", "rel_W", "rel_b",
                                 "logical_bias", "gate_W", "gate_b")]
_INS += [f"L0_ffn_{n}" for n in ("Wqkv", "q_scale", "k_scale", "Wo", "ln_g", "ln_b", "W1", "b1", "W2", "b2")]


def kernel(**inputs):
    import numpy as _np
    import concourse.bacc as _bacc
    from concourse import mybir as _mybir
    from concourse.bass_utils import run_bass_kernel_spmd as _run

    nc = _bacc.Bacc("TRN2", target_bir_lowering=False, num_devices=1)
    given = {name: _np.ascontiguousarray(inputs[name]) for name in _INS}
    given.update(global_constants())
    given.update(local_constants())
    arrays, args = {}, []
    for name, a in given.items():
        arrays[f"in_{name}"] = a
        args.append(nc.dram_tensor(f"in_{name}", a.shape, _mybir.dt.from_np(a.dtype), kind="ExternalInput").ap())
    out = nc.dram_tensor("out_x", [1, S, D], F32, kind="ExternalOutput").ap()
    program(nc, *args, out)
    return _run(nc, [arrays], core_ids=[0]).results[0]["out_x"]
```
